# Optimizing a Trainium2 kernel written in Bass

```python
import numpy as np
import jax
import jax.numpy as jnp

def _softmax(x, axis=-1):
    return jax.nn.softmax(x, axis=axis)

def _gelu(x):
    return jax.nn.gelu(x, approximate=True)

def _silu(x):
    return jax.nn.silu(x)

def _sigmoid(x):
    return jax.nn.sigmoid(x)

def _layernorm(x, axis=-1, eps=1e-05):
    m = jnp.mean(x, axis=axis, keepdims=True)
    v = jnp.var(x, axis=axis, keepdims=True)
    return (x - m) / jnp.sqrt(v + eps)

def _scatter_add(tgt, idx, src, axis=0):
    return tgt.at[idx].add(src)

def _segment_sum(src, seg, n):
    return jax.ops.segment_sum(src, seg, n)
kernel_name = 'mk_prb_d1_jaxref_r8_63418c'

def setup_inputs(seed: int=0):
    np.random.seed(seed)
    _w = jnp.asarray

    def _L0_attn_setup():
        import jax, jax.numpy as jnp
        import numpy as np
        import math
        D_MODEL = 128
        NUM_HEADS = 16
        THETA = 10000.0

        def _rope(x, theta):
            n, d_k = (x.shape[-2], x.shape[-1])
            powers = jnp.arange(0, d_k, 2, dtype=jnp.float32) / d_k
            freqs = 1.0 / theta ** powers
            t = jnp.arange(n, dtype=jnp.float32)
            angles = jnp.outer(t, freqs)
            cos = jnp.cos(angles).astype(x.dtype)
            sin = jnp.sin(angles).astype(x.dtype)
            x_even = x[..., 0::2]
            x_odd = x[..., 1::2]
            rot_even = x_even * cos - x_odd * sin
            rot_odd = x_even * sin + x_odd * cos
            return jnp.stack([rot_even, rot_odd], axis=-1).reshape(x.shape)
        key = jax.random.key(seed)
        ks = jax.random.split(key, 5)
        B, N, D = (2, 256, D_MODEL)
        std = math.sqrt(2.0 / (D + D))
        x = jax.random.normal(ks[0], (B, N, D), dtype=jnp.float32)
        wq = jax.random.normal(ks[1], (D, D), dtype=jnp.float32) * std
        wk = jax.random.normal(ks[2], (D, D), dtype=jnp.float32) * std
        wv = jax.random.normal(ks[3], (D, D), dtype=jnp.float32) * std
        wo = jax.random.normal(ks[4], (D, D), dtype=jnp.float32) * std
        return {'x': x, 'wq': wq, 'wk': wk, 'wv': wv, 'wo': wo}
    _L0_attn_in = _L0_attn_setup()

    def _L0_ffn_setup():
        import jax, jax.numpy as jnp
        import numpy as np
        B, S, K, N = (8, 1024, 128, 128)
        key = jax.random.key(seed)
        k1, k2, k3, k4 = jax.random.split(key, 4)
        x = jax.random.normal(k1, (B, S, K), dtype=jnp.float32)
        CB = jnp.clip(jnp.round(jax.random.normal(k2, (N, K), dtype=jnp.float32) * 42.0), -127.0, 127.0)
        SCB = jax.random.uniform(k3, (N,), dtype=jnp.float32, minval=0.5, maxval=2.0)
        bias = jax.random.normal(k4, (N,), dtype=jnp.float32) * 0.02
        return {'x': x, 'CB': CB, 'SCB': SCB, 'bias': bias}
    _L0_ffn_in = _L0_ffn_setup()
    _d = {'L0_attn_x': _L0_attn_in['x'], 'L0_attn_wq': _L0_attn_in['wq'], 'L0_attn_wk': _L0_attn_in['wk'], 'L0_attn_wv': _L0_attn_in['wv'], 'L0_attn_wo': _L0_attn_in['wo'], 'L0_ffn_CB': _L0_ffn_in['CB'], 'L0_ffn_SCB': _L0_ffn_in['SCB'], 'L0_ffn_bias': _L0_ffn_in['bias']}
    _x0 = _d['L0_attn_x']
    _d['L0_attn_x'] = jax.random.normal(jax.random.fold_in(jax.random.key(seed), 1), (2, 1024, 128), dtype=_x0.dtype)
    del _x0
    return _d

def reference(L0_attn_x, L0_attn_wq, L0_attn_wk, L0_attn_wv, L0_attn_wo, L0_ffn_CB, L0_ffn_SCB, L0_ffn_bias):

    def _L0_attn_ref(x, wq, wk, wv, wo):
        import jax, jax.numpy as jnp
        import numpy as np
        import math
        D_MODEL = 128
        NUM_HEADS = 16
        THETA = 10000.0

        def _rope(x, theta):
            n, d_k = (x.shape[-2], x.shape[-1])
            powers = jnp.arange(0, d_k, 2, dtype=jnp.float32) / d_k
            freqs = 1.0 / theta ** powers
            t = jnp.arange(n, dtype=jnp.float32)
            angles = jnp.outer(t, freqs)
            cos = jnp.cos(angles).astype(x.dtype)
            sin = jnp.sin(angles).astype(x.dtype)
            x_even = x[..., 0::2]
            x_odd = x[..., 1::2]
            rot_even = x_even * cos - x_odd * sin
            rot_odd = x_even * sin + x_odd * cos
            return jnp.stack([rot_even, rot_odd], axis=-1).reshape(x.shape)
        B, N, D = x.shape
        H = NUM_HEADS
        d_k = D // H

        def split_heads(t):
            return t.reshape(B, N, H, d_k).transpose(0, 2, 1, 3)
        Q = split_heads(x @ wq.T)
        K = split_heads(x @ wk.T)
        V = split_heads(x @ wv.T)
        Q = _rope(Q, THETA)
        K = _rope(K, THETA)
        scale = 1.0 / math.sqrt(d_k)
        scores = jnp.einsum('bhqd,bhkd->bhqk', Q, K) * scale
        causal_mask = jnp.triu(jnp.ones((N, N), dtype=bool), k=1)
        scores = jnp.where(causal_mask, -jnp.inf, scores)
        attn = jax.nn.softmax(scores, axis=-1)
        out = jnp.einsum('bhqk,bhkd->bhqd', attn, V)
        out = out.transpose(0, 2, 1, 3).reshape(B, N, D)
        return out @ wo.T

    def _L0_ffn_ref(x, CB, SCB, bias):
        import jax, jax.numpy as jnp
        import numpy as np
        B, S, K, N = (8, 1024, 128, 128)
        out = jnp.einsum('bsk,nk->bsn', x, CB)
        out = out * (SCB * (1.0 / 127.0)) + bias
        return out
    x = L0_attn_x
    xn = _layernorm(x, axis=-1)
    x = x + _L0_attn_ref(xn, L0_attn_wq, L0_attn_wk, L0_attn_wv, L0_attn_wo) + _L0_ffn_ref(xn, L0_ffn_CB, L0_ffn_SCB, L0_ffn_bias)
    return x

_drawn_inputs = setup_inputs


def setup_inputs(seed=0):
    import zlib

    import numpy as np

    out = dict(_drawn_inputs(seed))
    spreads = {}
    factors = {'L0_attn_wq': 2.761, 'L0_attn_wk': 2.711, 'L0_ffn_bias': 8.0}
    for name, (base, spread) in spreads.items():
        noise = np.random.default_rng([zlib.crc32(name.encode()), seed]).standard_normal(out[name].shape)
        drawn = base * np.exp(spread * noise) if base else spread * noise
        out[name] = jnp.asarray(drawn.astype(out[name].dtype))
    for name, factor in factors.items():
        out[name] = (out[name] * factor).astype(out[name].dtype)
    return out
```

```python
from contextlib import ExitStack

import numpy as np
import concourse.bass as bass
from concourse import mybir

P = 128
BATCH, SEQ, DM = 2, 1024, 128
HEADS, DH = 16, 8
TILES = BATCH * SEQ // P
TPB = SEQ // P
HALF = 512
QUAD = 4
QUADS = BATCH * HEADS // QUAD
SLOTS = 3
PARTS = 3
GROUP = PARTS * DH
STACK = PARTS * GROUP
SHIFT = STACK
NSHIFT = 2
SCALE = float(1.0 / np.sqrt(np.float32(DH)))
EPS = 1e-5
LOWEST = -3.0e38

F32 = mybir.dt.float32
BF16 = mybir.dt.bfloat16
ALU = mybir.AluOpType
ACT = mybir.ActivationFunctionType

FULL, D0, D1, D2 = range(4)
STEPS = [(D0, 0, 0), (D1, 0, None), (D2, 0, None)]
STEPS += [(FULL, 1, kb) for kb in range(4)]
STEPS += [(D0, 1, 4), (D1, 1, None), (D2, 1, None)]
NSTEPS = len(STEPS)
BANKS = [2 if kind == D2 else 4 for kind, _, _ in STEPS]
BANK_END = [sum(BANKS[:s + 1]) for s in range(NSTEPS)]
NBANKS = sum(BANKS)
MASKS = [{FULL: 0, D0: 1, D1: 2, D2: 1}[kind] for kind, _, _ in STEPS]
MASK_END = [sum(MASKS[:s + 1]) for s in range(NSTEPS)]
NMASKS = sum(MASKS)
LAST = {0: 2, 1: 9}
FIRST = {0: 0, 1: 3}
LAG = 2
B_RING = 3
P_RING = 5
UNITS = [(t, j) for t in range(TPB) for j in range(QUAD)]
NUNITS = len(UNITS)
HALF_UNITS = NUNITS // 2


def units_after():
    total = sum(t + 1 for t, _ in UNITS)
    out, u, work = [], 0, 0
    for n in range(NBANKS):
        k = 0
        while u < NUNITS and work + (UNITS[u][0] + 1) / 2 <= total * (n + 1) / NBANKS:
            work += UNITS[u][0] + 1
            u += 1
            k += 1
        out.append(k)
    out[-1] += NUNITS - u
    return out


def attention_ffn_kernel(nc, x, weights, rope, scb, bias, out):
    ctx = ExitStack()
    with ctx:
        def sb(name, shape, dt):
            return ctx.enter_context(nc.sbuf_tensor(name, shape, dt))

        def sem(name):
            return ctx.enter_context(nc.semaphore(name))

        x_sb = sb("x_sb", [P, TILES, DM], F32)
        xn = sb("xn", [P, TILES, DM], F32)
        xnT = sb("xnT", [P, TILES * P], F32)
        w_sb = sb("w_sb", [P, 7, DM], F32)
        rope_sb = sb("rope_sb", [P, 2, SEQ], F32)
        scb_sb = sb("scb_sb", [P, DM], F32)
        bias_sb = sb("bias_sb", [P, DM], F32)
        stats = sb("stats", [P, TILES, 6], F32)
        mv = sb("mv", [P, TILES, 2], F32)
        var_eps = sb("var_eps", [P, TILES], F32)
        exponent = sb("exponent", [P, TILES], F32)
        rstd = sb("rstd", [P, TILES], F32)
        ident = sb("ident", [P, P], F32)
        cmask = sb("cmask", [P, SEQ], F32)
        prod = sb("prod", [P, 2, 2, HALF], F32)
        rot = sb("rot", [P, 2, HALF], F32)
        rest = sb("rest", [P, 2, HALF], F32)
        parts = sb("parts", [P, 4, PARTS, HALF], BF16)
        v_all = sb("v_all", [P, TILES, DM], F32)
        va = sb("va", [P, TPB, QUAD, 32], F32)
        qs = sb("qs", [P, SLOTS, 2, QUAD, HALF], BF16)
        ks = sb("ks", [P, SLOTS, 2, QUAD, HALF], BF16)
        ring = sb("ring", [P, P_RING, QUAD * HALF], F32)
        mx = sb("mx", [P, 2, 16], F32)
        mrest = sb("mrest", [P, 2, 16], F32)
        shifts = sb("shifts", [P, 2, 32], BF16)
        shiftsT = sb("shiftsT", [P, 2, 32], BF16)
        ot = sb("ot", [P, QUADS, SEQ], F32)
        rden = sb("rden", [P, 2, HEADS], F32)
        on = sb("on", [P, 2, DM], F32)
        onT = sb("onT", [P, 2, DM], F32)
        masked_scores = prod[:, :, :, :].rearrange("p u m q -> p u (m q)")
        y_sb = xn

        psA = ctx.enter_context(nc.psum_tensor("psA", [P, 4 * HALF], F32))
        psB = ctx.enter_context(nc.psum_tensor("psB", [P, B_RING * HALF], F32))
        psV = ctx.enter_context(nc.psum_tensor("psV", [P, HALF], F32))

        scratch = nc.dram_tensor("scratch", [2, HEADS, 5, DH, BATCH * SEQ], BF16)

        def bank_a(n):
            return psA[:, n * HALF:(n + 1) * HALF]

        def bank_b(n):
            return psB[:, n * HALF:(n + 1) * HALF]

        def round_bank(r, w):
            if r % 2:
                return bank_a(w)
            return bank_b(w) if w < 3 else psV[:, :]

        x_in = [sem(f"x_in{b}") for b in range(BATCH)]
        w_in = sem("w_in")
        rope_in = sem("rope_in")
        vec_in = sem("vec_in")
        ident_ready = sem("ident_ready")
        cmask_ready = sem("cmask_ready")
        pads_ready = sem("pads_ready")
        wq_scaled = sem("wq_scaled")
        cb_scaled = sem("cb_scaled")
        ln_step = sem("ln_step")
        rstd_step = sem("rstd_step")
        rstd_ready = sem("rstd_ready")
        xn_ready = sem("xn_ready")
        xn_turned = sem("xn_turned")
        xnT_ready = sem("xnT_ready")
        projected = sem("projected")
        products = sem("products")
        rotated = sem("rotated")
        part1 = sem("part1")
        rest1 = sem("rest1")
        part2 = sem("part2")
        part3 = sem("part3")
        scratch_out = [sem(f"scratch_out{r}") for r in range(4)]
        v_projected = sem("v_projected")
        v_ready = sem("v_ready")
        xb_ready = sem("xb_ready")
        stack_in = [sem(f"stack_in{h}") for h in range(2)]
        a_filled = sem("a_filled")
        a_drained = sem("a_drained")
        split_step = sem("split_step")
        shift_split = sem("shift_split")
        shift_turned = [sem(f"shift_turned{h}") for h in range(2)]
        shift_in = [sem(f"shift_in{h}") for h in range(2)]
        b_filled = sem("b_filled")
        exp_done = sem("exp_done")
        masked = sem("masked")
        va_ready = sem("va_ready")
        pv_done = sem("pv_done")
        ot_saved = sem("ot_saved")
        o_turned = sem("o_turned")
        recip_ready = sem("recip_ready")
        on_ready = sem("on_ready")
        on_turned = sem("on_turned")
        onT_ready = sem("onT_ready")
        y_filled = sem("y_filled")
        y_ready = sem("y_ready")
        y_out = sem("y_out")
        passed = sem("passed")

        def wait(eng, semaphore, value, alone=False):
            if isinstance(value, int) and value <= 0:
                return
            eng.wait_ge(semaphore, value)
            if alone and not isinstance(value, int):
                eng.sem_inc(passed, 1)

        STACK_DMAS = 7
        SHIFT_DMAS = 8

        block = ctx.enter_context(nc.Block())

        @block.sync
        def _(sp):
            xv = x.rearrange("(t p) d -> p t d", p=P)
            for b in range(BATCH):
                sp.dma_start(x_sb[:, b * TPB:(b + 1) * TPB, :], xv[:, b * TPB:(b + 1) * TPB, :]).then_inc(x_in[b], 16)

            def store_parts(r):
                b, hf = divmod(r, 2)
                tok = b * SEQ + hf * HALF
                for w in range(2):
                    c = 2 * r + w
                    sp.wait_ge(part3, c + 1)
                    for p in range(5 if w == 0 else 3):
                        sp.dma_start(scratch[w, :, p, :, tok:tok + HALF],
                                     parts[:, c % 4, p % 3, :]).then_inc(scratch_out[r], 16)

            def load_stack(i, hf):
                slot, heads, tok = i % SLOTS, (i % 4) * QUAD, (i // 4) * SEQ + hf * HALF
                for g in range(PARTS):
                    for w, stack, p0 in ((0, qs, g), (1, ks, 0)):
                        sp.dma_start(stack[g * GROUP:(g + 1) * GROUP, bass.ds(slot, 1), hf, :, :].rearrange("r o h t -> r (o h) t"),
                                     scratch[w, bass.ds(heads, QUAD), p0:p0 + PARTS, :, bass.ds(tok, HALF)]
                                     .rearrange("h p d t -> (p d) h t")).then_inc(stack_in[hf], 16)
                sp.dma_start(qs[SHIFT:SHIFT + NSHIFT, bass.ds(slot, 1), hf, :, :].rearrange("r o h t -> r (o h) t"),
                             qs[SHIFT + NSHIFT:SHIFT + 2 * NSHIFT, bass.ds(slot, 1), hf, :, :].rearrange("r o h t -> r (o h) t"))\
                    .then_inc(stack_in[hf], 16)

            def store_shifts(i, hf):
                slot = i % SLOTS
                wait(sp, shift_turned[hf], i + 1, alone=True)
                for part in range(NSHIFT):
                    for blk in range(4):
                        dst = qs[SHIFT + part:SHIFT + part + 1, bass.ds(slot, 1), hf, :, :]
                        dst = dst.rearrange("r o h (t k q) -> r o (h t) k q", k=4, q=32)[:, :, :, blk, :]
                        sp.dma_start(dst, shiftsT[32 * blk + 16 * part:32 * blk + 16 * part + 16, hf, :])\
                            .then_inc(shift_in[hf], 16)

            for r in range(4):
                store_parts(r)
                sp.wait_ge(scratch_out[r], 16 * 8)
                if r == 0:
                    sp.wait_ge(pads_ready, 2)
                    load_stack(0, 0)
                if r == 1:
                    load_stack(0, 1)
                    for hf in range(2):
                        sp.wait_ge(stack_in[hf], 16 * STACK_DMAS)
                        load_stack(1, hf)
            store_shifts(0, 0)

            def body(i):
                for hf in range(2):
                    wait(sp, stack_in[hf], (i + 2) * (16 * STACK_DMAS), alone=True)
                wait(sp, b_filled, i * NBANKS, alone=True)
                for hf in range(2):
                    load_stack(i + 2, hf)
                store_shifts(i, 1)
                store_shifts(i + 1, 0)

            body(0)
            with sp.Fori(1, QUADS - 2) as i:
                body(i)
            store_shifts(6, 1)
            store_shifts(7, 0)
            store_shifts(7, 1)
            ov = out.rearrange("(t p) d -> p t d", p=P)
            for g in range(4):
                sp.wait_ge(y_ready, 4 * (g + 1))
                sp.dma_start(ov[:, 4 * g:4 * g + 4, :], y_sb[:, 4 * g:4 * g + 4, :]).then_inc(y_out, 16)
            sp.wait_ge(y_out, 16 * 4)

        @block.gpsimd
        def _(pool):
            pool.memset(ident[:, :], 0.0).then_inc(ident_ready, 1)
            pool.wait_ge(ident_ready, 1)
            pool.affine_select(out=ident[:, :], in_=ident[:, :], compare_op=ALU.not_equal, fill=1.0, base=0,
                               pattern=[[-1, P]], channel_multiplier=1).then_inc(ident_ready, 1)
            pool.memset(exponent[:, :], -0.5).then_inc(rstd_step, 1)
            for b in range(BATCH):
                pool.wait_ge(ln_step, 2 * b + 2)
                bt = slice(b * TPB, (b + 1) * TPB)
                pool.tensor_scalar(var_eps[:, bt], mv[:, bt, 1], EPS, None, ALU.add).then_inc(rstd_step, 1)
                pool.wait_ge(rstd_step, b + 2)
                pool.tensor_tensor(rstd[:, bt], var_eps[:, bt], exponent[:, bt], ALU.pow).then_inc(rstd_ready, 1)
            pool.memset(qs[:, :, :, :, :], 0.0).then_inc(pads_ready, 1)
            pool.memset(ks[:, :, :, :, :], 1.0).then_inc(pads_ready, 1)
            pool.memset(cmask[:, :], 0.0).then_inc(cmask_ready, 1)
            pool.wait_ge(cmask_ready, 1)
            pool.affine_select(out=cmask[:, SEQ - P:SEQ], in_=cmask[:, SEQ - P:SEQ], compare_op=ALU.is_ge,
                               fill=LOWEST, base=0, pattern=[[-1, P]], channel_multiplier=1).then_inc(cmask_ready, 1)
            pool.memset(va[:, :, :, :], 0.0).then_inc(cb_scaled, 1)
            pool.wait_ge(vec_in, 32)
            pool.wait_ge(w_in, 16)
            pool.tensor_scalar(scb_sb[:, :], scb_sb[:, :], 1.0 / 127.0, None, ALU.mult).then_inc(cb_scaled, 1)
            pool.wait_ge(cb_scaled, 2)
            pool.memset(va[:, :, :, DH:DH + 1], 1.0).then_inc(cb_scaled, 1)
            pool.tensor_tensor(w_sb[:, 6, :], w_sb[:, 6, :], scb_sb[:, :], ALU.mult).then_inc(cb_scaled, 1)

            for c in range(8):
                pool.wait_ge(part2, c + 1)
                if c >= 4:
                    pool.wait_ge(scratch_out[(c - 4) // 2], 16 * 8)
                pool.tensor_tensor(parts[:, c % 4, 2, :], rest[:, c % 2, :], parts[:, c % 4, 1, :],
                                   ALU.subtract).then_inc(part3, 1)
            pool.wait_ge(xn_ready, TILES)
            pool.tensor_tensor(x_sb[:, :, :], x_sb[:, :, :], bias_sb[:, :].unsqueeze(1).to_broadcast([P, TILES, DM]),
                               ALU.add).then_inc(xb_ready, 1)

            def split_maxima(i, hf):
                n = 2 * i + hf
                wait(pool, a_drained, i * NUNITS + (hf + 1) * HALF_UNITS)
                if hf == 0:
                    wait(pool, shift_turned[0], i, alone=True)
                else:
                    wait(pool, shift_turned[1], i, alone=True)
                pool.tensor_scalar(shifts[:, hf, 0:16], mx[:, hf, :], -1.0, None, ALU.mult).then_inc(split_step, 1)
                pool.wait_ge(split_step, 2 * n + 1)
                pool.tensor_tensor(mrest[:, hf, :], mx[:, hf, :], shifts[:, hf, 0:16], ALU.add).then_inc(split_step, 1)
                wait(pool, split_step, 2 * n + 2, alone=True)
                pool.tensor_scalar(shifts[:, hf, 16:32], mrest[:, hf, :], -1.0, None, ALU.mult).then_inc(shift_split, 1)

            def copy_v(i, hf):
                tiles, ch = (i // 4) * TPB + hf * 4, (i % 4) * (QUAD * DH)
                src = v_all[:, bass.ds(tiles, 4), bass.ds(ch, QUAD * DH)].rearrange("p t (h d) -> p t h d", d=DH)
                pool.tensor_copy(va[:, hf * 4:hf * 4 + 4, :, 0:DH], src).then_inc(va_ready, 1)

            def mask(i, s):
                kind = STEPS[s][0]
                buf = ring[:, s % P_RING, :]
                wait(pool, exp_done, i * NBANKS + BANK_END[s], alone=True)
                if kind == D2:
                    views = [buf[:, 0:QUAD * 256].rearrange("p (h q) -> p h q", h=QUAD)[:, :, 0:P]]
                else:
                    blocks = buf.rearrange("p (h k q) -> p h k q", h=QUAD, k=4)
                    views = [blocks[:, :, k, :] for k in ((0,) if kind == D0 else (0, 3))]
                for view in views:
                    pool.affine_select(out=view, in_=view, compare_op=ALU.is_ge, fill=0.0, base=0,
                                       pattern=[[0, QUAD], [1, P]], channel_multiplier=-1).then_inc(masked, 1)

            def body(i, more):
                split_maxima(i, 1)
                wait(pool, pv_done, i * NSTEPS - 3)
                copy_v(i, 0)
                mask(i, 0)
                mask(i, 1)
                wait(pool, pv_done, i * NSTEPS)
                copy_v(i, 1)
                mask(i, 2)
                if more:
                    split_maxima(i + 1, 0)
                mask(i, 7)
                mask(i, 8)
                mask(i, 9)

            split_maxima(0, 0)
            pool.wait_ge(v_ready, 4)
            body(0, True)
            with pool.Fori(1, QUADS - 1) as i:
                body(i, True)
            body(QUADS - 1, False)

        @block.scalar
        def _(act):
            act.dma_start(w_sb[:, :, :], weights).then_inc(w_in, 16)
            act.dma_start(rope_sb[:, :, :], rope).then_inc(rope_in, 16)
            act.dma_start(scb_sb[:, :], scb.partition_broadcast(P)).then_inc(vec_in, 16)
            act.dma_start(bias_sb[:, :], bias.partition_broadcast(P)).then_inc(vec_in, 16)
            act.wait_ge(w_in, 16)
            act.activation(w_sb[:, 0:2, :], w_sb[:, 0:2, :], ACT.Copy, scale=SCALE).then_inc(wq_scaled, 1)
            for g in range(4):
                act.wait_ge(xn_turned, g + 1)
                act.activation(xnT[:, g * HALF:(g + 1) * HALF], bank_a(g), ACT.Copy).then_inc(xnT_ready, 1)
            for c in range(9):
                if c < 8:
                    act.wait_ge(rotated, c + 1)
                    if c >= 4:
                        act.wait_ge(scratch_out[(c - 4) // 2], 16 * 8)
                    act.activation(parts[:, c % 4, 0, :], rot[:, c % 2, :], ACT.Copy).then_inc(part1, 1)
                if c >= 1:
                    act.wait_ge(rest1, c)
                    act.activation(parts[:, (c - 1) % 4, 1, :], rest[:, (c - 1) % 2, :], ACT.Copy).then_inc(part2, 1)
            for g in range(4):
                act.wait_ge(v_projected, g + 1)
                act.activation(v_all[:, 4 * g:4 * g + 4, :].rearrange("p t d -> p (t d)"), round_bank(4, g),
                               ACT.Copy).then_inc(v_ready, 1)

            def exps(i, s):
                wait(act, pv_done, i * NSTEPS + s - P_RING + 1)
                for n in range(BANK_END[s] - BANKS[s], BANK_END[s]):
                    k = n - (BANK_END[s] - BANKS[s])
                    wait(act, b_filled, i * NBANKS + n + 1)
                    act.activation(ring[:, s % P_RING, k * HALF:(k + 1) * HALF], bank_b(n % B_RING), ACT.Exp)\
                        .then_inc(exp_done, 1)

            def save(i, hf):
                wait(act, pv_done, i * NSTEPS + LAST[hf] + 1)
                act.activation(ot[:, bass.ds(i, 1), hf * HALF:(hf + 1) * HALF].rearrange("p o q -> p (o q)"),
                               psV[:, :], ACT.Copy).then_inc(ot_saved, 1)

            def body(i, first):
                for s in range(NSTEPS):
                    exps(i, s)
                    if s == LAG - 1 and not first:
                        save(i - 1, 1)
                    if s == LAST[0] + LAG:
                        save(i, 0)

            body(0, True)
            with act.Fori(1, QUADS) as i:
                body(i, False)
            save(QUADS - 1, 1)
            for t in range(TILES):
                act.wait_ge(on_turned, t + 1)
                if t >= 2:
                    act.wait_ge(y_filled, t - 1)
                act.activation(onT[:, t % 2, :], bank_b(t % 2)[:, 0:P], ACT.Copy).then_inc(onT_ready, 1)

        @block.vector
        def _(dve):
            n_ln = 0
            for b in range(BATCH):
                ts = range(b * TPB, (b + 1) * TPB)
                dve.wait_ge(x_in[b], 16)
                for t in ts:
                    last = dve.bn_stats(stats[:, t, :], x_sb[:, t, :])
                n_ln += 1
                last.then_inc(ln_step, 1)
                dve.wait_ge(ln_step, n_ln)
                for t in ts:
                    last = dve.bn_aggr(mv[:, t, :], stats[:, t, :])
                n_ln += 1
                last.then_inc(ln_step, 1)
                dve.wait_ge(ln_step, n_ln)
                dve.wait_ge(rstd_ready, b + 1)
                for t in ts:
                    dve.tensor_scalar(xn[:, t, :], x_sb[:, t, :], mv[:, t, 0:1], rstd[:, t:t + 1],
                                      ALU.subtract, ALU.mult).then_inc(xn_ready, 1)

            def leave(c):
                dve.wait_ge(part1, c + 1)
                if c >= 2:
                    dve.wait_ge(part3, c - 1)
                dve.tensor_tensor(rest[:, c % 2, :], rot[:, c % 2, :], parts[:, c % 4, 0, :],
                                  ALU.subtract).then_inc(rest1, 1)

            dve.wait_ge(rope_in, 16)
            for c in range(8):
                r, w = divmod(c, 2)
                cols = slice((r % 2) * HALF, (r % 2 + 1) * HALF)
                dve.wait_ge(projected, c + 1)
                for m in range(2):
                    dve.tensor_tensor(prod[:, c % 2, m, :], round_bank(r, 2 * w + m), rope_sb[:, m, cols],
                                      ALU.mult).then_inc(products, 1)
                dve.wait_ge(products, 2 * c + 2)
                dve.tensor_tensor(rot[:, c % 2, :], prod[:, c % 2, 0, :], prod[:, c % 2, 1, :],
                                  ALU.add).then_inc(rotated, 1)
                if c >= 1:
                    leave(c - 1)
            leave(7)

            def maximum(i, u):
                t, j = UNITS[u]
                w = (t + 1) * P
                wait(dve, a_filled, i * NUNITS + u + 1, alone=True)
                col = j * 4 + t % 4
                dve.tensor_tensor_reduce(masked_scores[:, u % 2, 0:w], psA[:, (u % 2) * SEQ:(u % 2) * SEQ + w],
                                         cmask[:, SEQ - w:SEQ], 1.0, LOWEST, ALU.add, ALU.max,
                                         mx[:, t // 4, col:col + 1]).then_inc(a_drained, 1)

            def turn_shifts(i, hf):
                wait(dve, shift_split, 2 * i + hf + 1)
                wait(dve, shift_in[hf], i * (16 * SHIFT_DMAS))
                dve.transpose(shiftsT[:, hf, :], shifts[:, hf, :]).then_inc(shift_turned[hf], 1)

            def body(i, more):
                if not more:
                    turn_shifts(i, 1)
                    return
                for u in range(NUNITS):
                    if u == 2:
                        turn_shifts(i, 1)
                    if u == HALF_UNITS + 3:
                        turn_shifts(i + 1, 0)
                    maximum(i + 1, u)

            dve.wait_ge(cmask_ready, 2)
            for u in range(NUNITS):
                if u == HALF_UNITS + 3:
                    turn_shifts(0, 0)
                maximum(0, u)
            body(0, True)
            with dve.Fori(1, QUADS - 1) as i:
                body(i, True)
            body(QUADS - 1, False)

            dve.wait_ge(xb_ready, 1)

            def result(t):
                dve.wait_ge(y_filled, t + 1)
                dve.tensor_tensor(y_sb[:, t, :], bank_b(2)[:, 0:P] if t % 2 else psV[:, 0:P], x_sb[:, t, :],
                                  ALU.add).then_inc(y_ready, 1)

            for t in range(TILES):
                dve.wait_ge(o_turned, t + 1)
                heads = bank_a(t % 4).rearrange("p (h c) -> p h c", c=32)
                if t >= 2:
                    dve.wait_ge(on_turned, t - 1)
                dve.reciprocal(rden[:, t % 2, :], heads[:, :, DH]).then_inc(recip_ready, 1)
                dve.wait_ge(recip_ready, t + 1)
                dve.tensor_tensor(on[:, t % 2, :].rearrange("p (h d) -> p h d", d=DH), heads[:, :, 0:DH],
                                  rden[:, t % 2, :].unsqueeze(2).to_broadcast([P, HEADS, DH]),
                                  ALU.mult).then_inc(on_ready, 1)
                if t >= 1:
                    result(t - 1)
            result(TILES - 1)

        @block.tensor
        def _(pe):
            pe.wait_ge(ident_ready, 2)
            for t in range(TILES):
                pe.wait_ge(xn_ready, t + 1)
                mm = pe.transpose(bank_a(t // 4)[:, (t % 4) * P:(t % 4 + 1) * P], xn[:, t, :], ident[:, :])
                if t % 4 == 3:
                    mm.then_inc(xn_turned, 1)
            pe.wait_ge(wq_scaled, 1)
            for r in range(4):
                pe.wait_ge(xnT_ready, 4 if r else 1)
                if r >= 2:
                    pe.wait_ge(products, 8 * (r - 1) - 4)
                for w in range(4):
                    mm = pe.matmul(round_bank(r, w), w_sb[:, w, :], xnT[:, r * HALF:(r + 1) * HALF],
                                   start=True, stop=True)
                    if w % 2:
                        mm.then_inc(projected, 1)
            pe.wait_ge(products, 12)
            for t in range(TILES):
                mm = pe.matmul(round_bank(4, t // 4)[:, (t % 4) * P:(t % 4 + 1) * P], xnT[:, t * P:(t + 1) * P],
                               w_sb[:, 4, :], start=True, stop=True)
                if t % 4 == 3:
                    mm.then_inc(v_projected, 1)

            def stack(tensor, i, j, start, size):
                half, at = divmod(start, HALF)
                return tensor[:, bass.ds(i % SLOTS, 1), half, j, at:at + size].rearrange("p o t -> p (o t)")

            def scores(i, u):
                t, j = UNITS[u]
                if u in (0, HALF_UNITS):
                    wait(pe, stack_in[u // HALF_UNITS], (i + 1) * (16 * STACK_DMAS))
                wait(pe, a_drained, i * NUNITS + u - 1)
                w = (t + 1) * P
                for k in range(0, w, HALF):
                    mm = pe.matmul(psA[:, (u % 2) * SEQ + k:(u % 2) * SEQ + min(k + HALF, w)],
                                   stack(qs, i, j, t * P, P), stack(ks, i, j, k, min(HALF, w - k)),
                                   start=True, stop=True)
                mm.then_inc(a_filled, 1)

            def shifted(i, s, k):
                kind, hf, kb = STEPS[s]
                n = BANK_END[s] - BANKS[s] + k
                out_bank = bank_b(n % B_RING)
                wait(pe, exp_done, i * NBANKS + n - B_RING + 1)
                if k == 0 and s == FIRST[hf]:
                    wait(pe, shift_in[hf], (i + 1) * (16 * SHIFT_DMAS))
                if kind in (FULL, D0):
                    pieces = [(0, k, kb, 0)]
                elif kind == D1:
                    pieces = [(0, k, 4 * hf + 1, P), (3 * P, k, 4 * hf + 3, 3 * P)]
                else:
                    pieces = [(0, 2 * k, 4 * hf + 2, 2 * P), (2 * P, 2 * k + 1, 4 * hf + 2, 2 * P)]
                for col, j, b, q0 in pieces:
                    size = HALF - q0
                    mm = pe.matmul(out_bank[:, col:col + size], stack(ks, i, j, b * P, P),
                                   stack(qs, i, j, hf * HALF + q0, size), start=True, stop=True)
                mm.then_inc(b_filled, 1)

            def values(i, s):
                kind, hf, kb = STEPS[s]
                if kind == FULL:
                    wait(pe, exp_done, i * NBANKS + BANK_END[s])
                else:
                    wait(pe, masked, i * NMASKS + MASK_END[s])
                if s == FIRST[hf]:
                    wait(pe, ot_saved, 2 * i + hf)
                if s == 0 or s == 7:
                    wait(pe, va_ready, 2 * i + (s == 7) + 1)
                if kind in (FULL, D0):
                    pieces = [(kb, 0, HALF, 0)]
                elif kind == D1:
                    pieces = [(4 * hf + 1, P, HALF, 0), (4 * hf + 3, 3 * P, HALF, 3 * P)]
                else:
                    pieces = [(4 * hf + 2, 2 * P, 256, 0)]
                for b, q0, pitch, at in pieces:
                    for j in range(QUAD):
                        src = ring[:, s % P_RING, j * pitch + at:j * pitch + at + HALF - q0]
                        mm = pe.matmul(psV[32 * j:32 * j + 32, q0:HALF], va[:, b, j, :], src,
                                       start=(s == FIRST[hf]), stop=(s == LAST[hf]))
                mm.then_inc(pv_done, 1)

            after = units_after()

            def body(i, first, more):
                u = 0
                for s in range(NSTEPS):
                    for k in range(BANKS[s]):
                        shifted(i, s, k)
                        if k == 1:
                            if s >= LAG:
                                values(i, s - LAG)
                            elif not first:
                                values(i - 1, NSTEPS + s - LAG)
                        if more:
                            for _ in range(after[BANK_END[s] - BANKS[s] + k]):
                                scores(i + 1, u)
                                u += 1

            pe.wait_ge(products, 16)
            for u in range(NUNITS):
                scores(0, u)
            pe.wait_ge(v_ready, 4)
            body(0, True, True)
            with pe.Fori(1, QUADS - 1) as i:
                body(i, False, True)
            body(QUADS - 1, False, False)
            for s in range(NSTEPS - LAG, NSTEPS):
                values(QUADS - 1, s)

            def turn(t):
                b, q = divmod(t, TPB)
                if t >= 4:
                    pe.wait_ge(on_ready, t - 3)
                for k in range(4):
                    mm = pe.transpose(bank_a(t % 4)[:, k * P:(k + 1) * P], ot[:, 4 * b + k, q * P:(q + 1) * P],
                                      ident[:, :])
                mm.then_inc(o_turned, 1)

            def turn_back(t):
                pe.wait_ge(on_ready, t + 1)
                if t >= 2:
                    pe.wait_ge(onT_ready, t - 1)
                pe.transpose(bank_b(t % 2)[:, 0:P], on[:, t % 2, :], ident[:, :]).then_inc(on_turned, 1)

            def project(t):
                pe.wait_ge(onT_ready, t + 1)
                if t >= 2:
                    pe.wait_ge(y_ready, t - 1)
                dst = bank_b(2)[:, 0:P] if t % 2 else psV[:, 0:P]
                pe.matmul(dst, xnT[:, t * P:(t + 1) * P], w_sb[:, 6, :], start=True, stop=False)
                pe.matmul(dst, onT[:, t % 2, :], w_sb[:, 5, :], start=False, stop=True).then_inc(y_filled, 1)

            pe.wait_ge(ot_saved, 2 * QUADS)
            pe.wait_ge(cb_scaled, 4)
            for t in range(TILES + 2):
                if t < TILES:
                    turn(t)
                if 1 <= t <= TILES:
                    turn_back(t - 1)
                if t >= 2:
                    project(t - 2)


def rope_tables():
    powers = np.arange(0, DH, 2, dtype=np.float32) / np.float32(DH)
    freqs = (np.float32(1.0) / np.power(np.float32(10000.0), powers)).astype(np.float32)
    angles = np.outer(np.arange(SEQ, dtype=np.float32), freqs).astype(np.float32)
    cos, sin = np.cos(angles), np.sin(angles)
    table = np.empty((P, 2, SEQ), np.float32)
    for ch in range(P):
        f = (ch % DH) // 2
        table[ch, 0] = cos[:, f]
        table[ch, 1] = sin[:, f] if ch % 2 else -sin[:, f]
    return table


def kernel(L0_attn_x, L0_attn_wq, L0_attn_wk, L0_attn_wv, L0_attn_wo, L0_ffn_CB, L0_ffn_SCB, L0_ffn_bias):
    import concourse.bacc as bacc
    from concourse.bass_utils import run_bass_kernel_spmd

    swap = np.arange(P) ^ 1
    wq, wk = np.asarray(L0_attn_wq), np.asarray(L0_attn_wk)
    weights = np.stack([wq.T, wq[swap].T, wk.T, wk[swap].T, np.asarray(L0_attn_wv).T,
                        np.asarray(L0_attn_wo).T, np.asarray(L0_ffn_CB).T], axis=1)
    arrays = {
        "x": np.ascontiguousarray(L0_attn_x).reshape(BATCH * SEQ, DM),
        "weights": np.ascontiguousarray(weights),
        "rope": rope_tables(),
        "scb": np.ascontiguousarray(L0_ffn_SCB),
        "bias": np.ascontiguousarray(L0_ffn_bias),
    }
    nc = bacc.Bacc("TRN2", target_bir_lowering=False, num_devices=1)
    args = [nc.dram_tensor(n, a.shape, mybir.dt.from_np(a.dtype), kind="ExternalInput").ap() for n, a in arrays.items()]
    y = nc.dram_tensor("y", (BATCH * SEQ, DM), F32, kind="ExternalOutput").ap()
    attention_ffn_kernel(nc, *args, y)
    r = run_bass_kernel_spmd(nc, [arrays], core_ids=[0])
    return r.results[0]["y"].reshape(BATCH, SEQ, DM)
```

```python
from contextlib import ExitStack

import numpy as np
import concourse.bass as bass
from concourse import mybir

P = 128
BATCH, SEQ, DM = 2, 1024, 128
HEADS, DH = 16, 8
TILES = BATCH * SEQ // P
TPB = SEQ // P
HALF = 512
QUAD = 4
QUADS = BATCH * HEADS // QUAD
SLOTS = 3
PARTS = 3
GROUP = PARTS * DH
STACK = PARTS * GROUP
SHIFT = STACK
NSHIFT = 2
SCALE = float(1.0 / np.sqrt(np.float32(DH)))
EPS = 1e-5
LOWEST = -3.0e38
TWO_ONES = float(np.frombuffer(np.array([0x3F803F80], np.uint32).tobytes(), np.float32)[0])

F32 = mybir.dt.float32
BF16 = mybir.dt.bfloat16
ALU = mybir.AluOpType
ACT = mybir.ActivationFunctionType

FULL, D0, D1, D2 = range(4)
STEPS = [(D0, 0, 0), (D1, 0, None), (D2, 0, None)]
STEPS += [(FULL, 1, kb) for kb in range(4)]
STEPS += [(D0, 1, 4), (D1, 1, None), (D2, 1, None)]
NSTEPS = len(STEPS)
BANKS = [2 if kind == D2 else 4 for kind, _, _ in STEPS]
BANK_END = [sum(BANKS[:s + 1]) for s in range(NSTEPS)]
NBANKS = sum(BANKS)
MASKS = [{FULL: 0, D0: 1, D1: 2, D2: 1}[kind] for kind, _, _ in STEPS]
MASK_END = [sum(MASKS[:s + 1]) for s in range(NSTEPS)]
NMASKS = sum(MASKS)
LAST = {0: 2, 1: 9}
FIRST = {0: 0, 1: 3}
LAG = 2
B_RING = 3
P_RING = 5
UNITS = []
for t in range(TPB):
    together = {0: 4, 1: 4, 2: 2, 3: 2}.get(t, 1)
    UNITS += [(t, range(j, j + together)) for j in range(0, QUAD, together)]
NUNITS = len(UNITS)
HALF_UNITS = sum(t < TPB // 2 for t, _ in UNITS)


def units_after():
    blocks = [(t + 1) * len(heads) for t, heads in UNITS]
    out, u, work = [], 0, 0
    for n in range(NBANKS):
        k = 0
        while u < NUNITS and work + blocks[u] / 2 <= sum(blocks) * (n + 1) / NBANKS:
            work += blocks[u]
            u += 1
            k += 1
        out.append(k)
    out[-1] += NUNITS - u
    return out


def unit_place(u, j):
    t, heads = UNITS[u]
    w = (t + 1) * P
    pitch = HALF if len(heads) == 2 else 256 if t == 1 else w
    return (j - heads[0]) * pitch, w


GROUPS = TILES // 2
EARLY = {2: 0, 8: 1, 14: 2, 20: 3, 26: 4, 31: 5}
TURN_BACK, PROJECT = 2, 4


def attention_ffn_kernel(nc, x, weights, rope, scb, bias, out):
    ctx = ExitStack()
    with ctx:
        def sb(name, shape, dt):
            return ctx.enter_context(nc.sbuf_tensor(name, shape, dt))

        def sem(name):
            return ctx.enter_context(nc.semaphore(name))

        x_sb = sb("x_sb", [P, TILES, DM], F32)
        xn = sb("xn", [P, TILES, DM], F32)
        xnT = sb("xnT", [P, TILES * P], F32)
        w_sb = sb("w_sb", [P, 7, DM], F32)
        rope_sb = sb("rope_sb", [P, 2, SEQ], F32)
        scb_sb = sb("scb_sb", [P, DM], F32)
        bias_sb = sb("bias_sb", [P, DM], F32)
        stats = sb("stats", [P, TILES, 6], F32)
        mv = sb("mv", [P, TILES, 2], F32)
        var_eps = sb("var_eps", [P, TILES], F32)
        exponent = sb("exponent", [P, TILES], F32)
        rstd = sb("rstd", [P, TILES], F32)
        ident = sb("ident", [P, P], F32)
        cmask = sb("cmask", [P, SEQ], F32)
        prod = sb("prod", [P, 2, 2, HALF], F32)
        rot = sb("rot", [P, 2, HALF], F32)
        rest = sb("rest", [P, 2, HALF], F32)
        v_all = sb("v_all", [P, TILES, DM], F32)
        va = sb("va", [P, TPB, QUAD, 32], F32)
        qs = sb("qs", [P, SLOTS, 2, QUAD, HALF], BF16)
        ks = sb("ks", [P, SLOTS, 2, QUAD, HALF], BF16)
        ring = sb("ring", [P, P_RING, QUAD * HALF], F32)
        mx = sb("mx", [P, 2, 16], F32)
        mrest = sb("mrest", [P, 2, 16], F32)
        shifts = sb("shifts", [P, 2, 32], BF16)
        shiftsT = sb("shiftsT", [P, 2, 32], BF16)
        ot = sb("ot", [P, QUADS, SEQ], F32)
        rden = sb("rden", [P, 2, 2 * HEADS], F32)
        on = sb("on", [P, 2, 2 * DM], F32)
        onT = sb("onT", [P, 2, 2 * DM], F32)
        parts = ot[:, QUADS // 2:, :].rearrange("p a b -> p (a b)").bitcast(BF16)\
            .rearrange("p (r n t) -> p r n t", r=2, t=HALF)

        def part(c, n):
            return parts[:, (c // 2) % 2, 5 * (c % 2) + n, :]

        masked_scores = prod[:, :, :, :].rearrange("p u m q -> p u (m q)")
        y_sb = xn

        psA = ctx.enter_context(nc.psum_tensor("psA", [P, 4 * HALF], F32))
        psB = ctx.enter_context(nc.psum_tensor("psB", [P, B_RING * HALF], F32))
        psV = ctx.enter_context(nc.psum_tensor("psV", [P, HALF], F32))

        scratch = nc.dram_tensor("scratch", [4, HEADS, DH, PARTS, BATCH * SEQ], BF16)

        def bank_a(n):
            return psA[:, n * HALF:(n + 1) * HALF]

        def bank_b(n):
            return psB[:, n * HALF:(n + 1) * HALF]

        def round_bank(r, w):
            if r % 2:
                return bank_a(w)
            return bank_b(w) if w < 3 else psV[:, :]

        def result_bank(g, n):
            if g < GROUPS - 1:
                return bank_a(n)
            return bank_b(n) if n < 3 else psV[:, :]

        x_in = [sem(f"x_in{g}") for g in range(4)]
        w_in = sem("w_in")
        rope_in = sem("rope_in")
        vec_in = sem("vec_in")
        ident_ready = sem("ident_ready")
        cmask_ready = sem("cmask_ready")
        pads_ready = sem("pads_ready")
        wq_scaled = sem("wq_scaled")
        cb_scaled = sem("cb_scaled")
        ln_step = sem("ln_step")
        rstd_step = sem("rstd_step")
        rstd_ready = sem("rstd_ready")
        xn_ready = sem("xn_ready")
        xn_turned = sem("xn_turned")
        xnT_ready = sem("xnT_ready")
        projected = sem("projected")
        products = sem("products")
        rotated = sem("rotated")
        part1 = sem("part1")
        rest1 = sem("rest1")
        part2 = sem("part2")
        part3 = sem("part3")
        part_again = sem("part_again")
        scratch_out = [sem(f"scratch_out{r}") for r in range(4)]
        v_projected = sem("v_projected")
        v_ready = sem("v_ready")
        xb_ready = sem("xb_ready")
        stack_in = [sem(f"stack_in{h}") for h in range(2)]
        a_filled = sem("a_filled")
        a_drained = sem("a_drained")
        split_step = sem("split_step")
        shift_split = sem("shift_split")
        shift_turned = [sem(f"shift_turned{h}") for h in range(2)]
        shift_in = [sem(f"shift_in{h}") for h in range(2)]
        b_filled = sem("b_filled")
        exp_done = sem("exp_done")
        masked = sem("masked")
        va_ready = sem("va_ready")
        pv_done = sem("pv_done")
        ot_saved = sem("ot_saved")
        o_turned = sem("o_turned")
        recip_ready = sem("recip_ready")
        on_ready = sem("on_ready")
        on_turned = sem("on_turned")
        onT_ready = sem("onT_ready")
        y_filled = sem("y_filled")
        y_ready = sem("y_ready")
        y_out = sem("y_out")
        passed = sem("passed")

        def wait(eng, semaphore, value, alone=False):
            if isinstance(value, int) and value <= 0:
                return
            eng.wait_ge(semaphore, value)
            if alone and not isinstance(value, int):
                eng.sem_inc(passed, 1)

        STACK_DMAS = 7
        SHIFT_DMAS = 4
        ROUND_DMAS = 4

        block = ctx.enter_context(nc.Block())

        @block.sync
        def _(sp):
            xv = x.rearrange("(t p) d -> p t d", p=P)
            for g in range(4):
                sp.dma_start(x_sb[:, 4 * g:4 * g + 4, :], xv[:, 4 * g:4 * g + 4, :]).then_inc(x_in[g], 16)

            def store_parts(r):
                b, hf = divmod(r, 2)
                tok = b * SEQ + hf * HALF
                for w in range(4):
                    c = 2 * r + (w == 3)
                    sp.wait_ge(part3, c + 1)
                    if w < 3:
                        sp.wait_ge(part_again, 2 * r + 2)
                    n = w if w < 3 else 5
                    sp.dma_start(scratch[w, :, :, :, tok:tok + HALF].rearrange("h d p t -> (h d) p t"),
                                 parts[:, r % 2, n:n + PARTS, :]).then_inc(scratch_out[r], 16)

            def load_stack(i, hf):
                slot, heads, tok = i % SLOTS, (i % 4) * QUAD, (i // 4) * SEQ + hf * HALF
                for g in range(PARTS):
                    for w, stack in ((g, qs), (3, ks)):
                        sp.dma_start(stack[g * GROUP:(g + 1) * GROUP, bass.ds(slot, 1), hf, :, :].rearrange("r o h t -> r (o h) t"),
                                     scratch[w, bass.ds(heads, QUAD), :, :, bass.ds(tok, HALF)]
                                     .rearrange("h d p t -> (d p) h t")).then_inc(stack_in[hf], 16)
                sp.dma_start(qs[SHIFT:SHIFT + NSHIFT, bass.ds(slot, 1), hf, :, :].rearrange("r o h t -> r (o h) t"),
                             qs[SHIFT + NSHIFT:SHIFT + 2 * NSHIFT, bass.ds(slot, 1), hf, :, :].rearrange("r o h t -> r (o h) t"))\
                    .then_inc(stack_in[hf], 16)

            def store_shifts(i, hf):
                slot = i % SLOTS
                wait(sp, shift_turned[hf], i + 1, alone=True)
                for blk in range(4):
                    dst = qs[SHIFT:SHIFT + NSHIFT, bass.ds(slot, 1), hf, :, :]
                    dst = dst.rearrange("r o h (t k q) -> r o (h t) k q", k=4, q=32)[:, :, :, blk, :]
                    sp.dma_start(dst, shiftsT[32 * blk:32 * blk + 32, hf, :]).then_inc(shift_in[hf], 16)

            for hf in range(2):
                store_parts(hf)
                sp.wait_ge(scratch_out[hf], 16 * ROUND_DMAS)
                sp.wait_ge(pads_ready, 2)
                load_stack(0, hf)
            sp.wait_ge(pads_ready, 4)
            for hf in range(2):
                sp.wait_ge(stack_in[hf], 16 * STACK_DMAS)
                load_stack(1, hf)
            store_shifts(0, 0)
            for r in range(2, 4):
                store_parts(r)
            for r in range(2, 4):
                sp.wait_ge(scratch_out[r], 16 * ROUND_DMAS)
            sp.wait_ge(pads_ready, 6)

            def body(i):
                store_shifts(i, 1)
                for hf in range(2):
                    wait(sp, stack_in[hf], (i + 2) * (16 * STACK_DMAS), alone=True)
                wait(sp, b_filled, i * NBANKS, alone=True)
                for hf in range(2):
                    load_stack(i + 2, hf)
                store_shifts(i + 1, 0)

            body(0)
            with sp.Fori(1, QUADS - 2) as i:
                body(i)
            store_shifts(6, 1)
            store_shifts(7, 0)
            store_shifts(7, 1)
            ov = out.rearrange("(t p) d -> p t d", p=P)
            for g in range(GROUPS):
                sp.wait_ge(y_ready, g + 1)
                sp.dma_start(ov[:, 2 * g:2 * g + 2, :], y_sb[:, 2 * g:2 * g + 2, :]).then_inc(y_out, 16)
            sp.wait_ge(y_out, 16 * GROUPS)

        @block.gpsimd
        def _(pool):
            pool.memset(ident[:, :], 0.0).then_inc(ident_ready, 1)
            pool.wait_ge(ident_ready, 1)
            pool.affine_select(out=ident[:, :], in_=ident[:, :], compare_op=ALU.not_equal, fill=1.0, base=0,
                               pattern=[[-1, P]], channel_multiplier=1).then_inc(ident_ready, 1)
            pool.memset(exponent[:, :], -0.5).then_inc(rstd_step, 1)

            def pads(slot):
                pool.memset(qs[:, slot, :, :, :].rearrange("p a h t -> p (a h t)").bitcast(F32), 0.0)\
                    .then_inc(pads_ready, 1)
                pool.memset(ks[:, slot, :, :, :].rearrange("p a h t -> p (a h t)").bitcast(F32), TWO_ONES)\
                    .then_inc(pads_ready, 1)

            pads(0)
            for g in range(4):
                bt = slice(4 * g, 4 * g + 4)
                pool.wait_ge(ln_step, 2 * g + 2)
                pool.tensor_scalar(var_eps[:, bt], mv[:, bt, 1], EPS, None, ALU.add).then_inc(rstd_step, 1)
                pool.wait_ge(rstd_step, g + 2)
                pool.tensor_tensor(rstd[:, bt], var_eps[:, bt], exponent[:, bt], ALU.pow).then_inc(rstd_ready, 1)
            pool.memset(cmask[:, :], 0.0).then_inc(cmask_ready, 1)
            pool.wait_ge(cmask_ready, 1)
            pool.affine_select(out=cmask[:, SEQ - P:SEQ], in_=cmask[:, SEQ - P:SEQ], compare_op=ALU.is_ge,
                               fill=LOWEST, base=0, pattern=[[-1, P]], channel_multiplier=1).then_inc(cmask_ready, 1)

            def third_part(c):
                pool.wait_ge(part2, c + 1)
                if c >= 4:
                    pool.wait_ge(scratch_out[c // 2 - 2], 16 * ROUND_DMAS)
                pool.tensor_tensor(part(c, 2), rest[:, c % 2, :], part(c, 1), ALU.subtract).then_inc(part3, 1)

            for c in range(4):
                third_part(c)
            pads(1)
            for c in range(4, 8):
                third_part(c)
            pads(2)
            pool.memset(va[:, :, :, :], 0.0).then_inc(cb_scaled, 1)
            pool.wait_ge(vec_in, 32)
            pool.wait_ge(w_in, 16)
            pool.tensor_scalar(scb_sb[:, :], scb_sb[:, :], 1.0 / 127.0, None, ALU.mult).then_inc(cb_scaled, 1)
            pool.wait_ge(cb_scaled, 2)
            pool.memset(va[:, :, :, DH:DH + 1], 1.0).then_inc(cb_scaled, 1)
            pool.tensor_tensor(w_sb[:, 6, :], w_sb[:, 6, :], scb_sb[:, :], ALU.mult).then_inc(cb_scaled, 1)

            def split_maxima(i, hf):
                n = 2 * i + hf
                wait(pool, a_drained, i * NUNITS + (NUNITS if hf else HALF_UNITS))
                if hf == 0:
                    wait(pool, shift_turned[0], i, alone=True)
                else:
                    wait(pool, shift_turned[1], i, alone=True)
                pool.tensor_scalar(shifts[:, hf, 0:16], mx[:, hf, :], -1.0, None, ALU.mult).then_inc(split_step, 1)
                pool.wait_ge(split_step, 2 * n + 1)
                pool.tensor_tensor(mrest[:, hf, :], mx[:, hf, :], shifts[:, hf, 0:16], ALU.add).then_inc(split_step, 1)
                wait(pool, split_step, 2 * n + 2, alone=True)
                pool.tensor_scalar(shifts[:, hf, 16:32], mrest[:, hf, :], -1.0, None, ALU.mult).then_inc(shift_split, 1)

            def copy_v(i, hf):
                tiles, ch = (i // 4) * TPB + hf * 4, (i % 4) * (QUAD * DH)
                src = v_all[:, bass.ds(tiles, 4), bass.ds(ch, QUAD * DH)].rearrange("p t (h d) -> p t h d", d=DH)
                pool.tensor_copy(va[:, hf * 4:hf * 4 + 4, :, 0:DH], src).then_inc(va_ready, 1)

            def mask(i, s):
                kind = STEPS[s][0]
                buf = ring[:, s % P_RING, :]
                wait(pool, exp_done, i * NBANKS + BANK_END[s], alone=True)
                if kind == D2:
                    views = [buf[:, 0:QUAD * 256].rearrange("p (h q) -> p h q", h=QUAD)[:, :, 0:P]]
                else:
                    blocks = buf.rearrange("p (h k q) -> p h k q", h=QUAD, k=4)
                    views = [blocks[:, :, k, :] for k in ((0,) if kind == D0 else (0, 3))]
                for view in views:
                    pool.affine_select(out=view, in_=view, compare_op=ALU.is_ge, fill=0.0, base=0,
                                       pattern=[[0, QUAD], [1, P]], channel_multiplier=-1).then_inc(masked, 1)

            def body(i, more):
                split_maxima(i, 1)
                wait(pool, pv_done, i * NSTEPS - 3)
                copy_v(i, 0)
                mask(i, 0)
                mask(i, 1)
                wait(pool, pv_done, i * NSTEPS)
                copy_v(i, 1)
                mask(i, 2)
                if more:
                    split_maxima(i + 1, 0)
                mask(i, 7)
                mask(i, 8)
                mask(i, 9)

            split_maxima(0, 0)
            pool.wait_ge(xn_ready, TILES)
            pool.tensor_tensor(x_sb[:, :, :], x_sb[:, :, :], bias_sb[:, :].unsqueeze(1).to_broadcast([P, TILES, DM]),
                               ALU.add).then_inc(xb_ready, 1)
            pool.wait_ge(v_ready, 4)
            body(0, True)
            with pool.Fori(1, QUADS - 1) as i:
                body(i, True)
            body(QUADS - 1, False)

        @block.scalar
        def _(act):
            act.dma_start(w_sb[:, :, :], weights).then_inc(w_in, 16)
            act.dma_start(rope_sb[:, :, :], rope).then_inc(rope_in, 16)
            act.dma_start(scb_sb[:, :], scb.partition_broadcast(P)).then_inc(vec_in, 16)
            act.dma_start(bias_sb[:, :], bias.partition_broadcast(P)).then_inc(vec_in, 16)
            act.wait_ge(w_in, 16)
            act.activation(w_sb[:, 0:2, :], w_sb[:, 0:2, :], ACT.Copy, scale=SCALE).then_inc(wq_scaled, 1)
            for g in range(4):
                act.wait_ge(xn_turned, g + 1)
                act.activation(xnT[:, g * HALF:(g + 1) * HALF], bank_a(g), ACT.Copy).then_inc(xnT_ready, 1)
            def parts_of(c, source, n):
                act.activation(part(c, n), source[:, c % 2, :], ACT.Copy).then_inc((part1, part2)[n], 1)

            def again(c, n):
                if c % 2 == 0:
                    act.activation(part(c, 3 + n), (rot, rest)[n][:, c % 2, :], ACT.Copy).then_inc(part_again, 1)

            for c in range(9):
                if c < 8:
                    act.wait_ge(rotated, c + 1)
                    if c >= 4:
                        act.wait_ge(scratch_out[c // 2 - 2], 16 * ROUND_DMAS)
                    parts_of(c, rot, 0)
                    again(c, 0)
                if c >= 1:
                    act.wait_ge(rest1, c)
                    parts_of(c - 1, rest, 1)
                    again(c - 1, 1)
            for g in range(4):
                act.wait_ge(v_projected, g + 1)
                act.activation(v_all[:, 4 * g:4 * g + 4, :].rearrange("p t d -> p (t d)"), round_bank(4, g),
                               ACT.Copy).then_inc(v_ready, 1)

            def exps(i, s, then=None):
                wait(act, pv_done, i * NSTEPS + s - P_RING + 1)
                for n in range(BANK_END[s] - BANKS[s], BANK_END[s]):
                    k = n - (BANK_END[s] - BANKS[s])
                    wait(act, b_filled, i * NBANKS + n + 1)
                    act.activation(ring[:, s % P_RING, k * HALF:(k + 1) * HALF], bank_b(n % B_RING), ACT.Exp)\
                        .then_inc(exp_done, 1)
                    if then:
                        then(n)

            def save(i, hf):
                wait(act, pv_done, i * NSTEPS + LAST[hf] + 1)
                act.activation(ot[:, bass.ds(i, 1), hf * HALF:(hf + 1) * HALF].rearrange("p o q -> p (o q)"),
                               psV[:, :], ACT.Copy).then_inc(ot_saved, 1)

            def body(i, first):
                for s in range(NSTEPS):
                    exps(i, s)
                    if s == LAG - 1 and not first:
                        save(i - 1, 1)
                    if s == LAST[0] + LAG:
                        save(i, 0)

            def copy_turned(g):
                act.wait_ge(on_turned, g + 1)
                if g >= 2:
                    act.wait_ge(y_filled, g - 1)
                act.activation(onT[:, g % 2, :], result_bank(g, 2)[:, 0:2 * P], ACT.Copy).then_inc(onT_ready, 1)

            body(0, True)
            with act.Fori(1, QUADS - 1) as i:
                body(i, False)
            last = QUADS - 1
            for s in range(NSTEPS):
                exps(last, s, then=lambda n: copy_turned(EARLY[n - TURN_BACK]) if n - TURN_BACK in EARLY else None)
                if s == LAG - 1:
                    save(last - 1, 1)
                if s == LAST[0] + LAG:
                    save(last, 0)
            save(last, 1)
            for g in range(len(EARLY), GROUPS):
                copy_turned(g)

        @block.vector
        def _(dve):
            def statistics(g):
                dve.wait_ge(x_in[g], 16)
                for t in range(4 * g, 4 * g + 4):
                    last = dve.bn_stats(stats[:, t, :], x_sb[:, t, :])
                last.then_inc(ln_step, 1)
                dve.wait_ge(ln_step, 2 * g + 1)
                for t in range(4 * g, 4 * g + 4):
                    last = dve.bn_aggr(mv[:, t, :], stats[:, t, :])
                last.then_inc(ln_step, 1)

            def normalise(g):
                dve.wait_ge(rstd_ready, g + 1)
                for t in range(4 * g, 4 * g + 4):
                    dve.tensor_scalar(xn[:, t, :], x_sb[:, t, :], mv[:, t, 0:1], rstd[:, t:t + 1],
                                      ALU.subtract, ALU.mult).then_inc(xn_ready, 1)

            statistics(0)
            for g in range(4):
                if g < 3:
                    statistics(g + 1)
                normalise(g)

            def leave(c):
                dve.wait_ge(part1, c + 1)
                if c >= 2:
                    dve.wait_ge(part3, c - 1)
                    if c % 2 == 0:
                        dve.wait_ge(part_again, c)
                dve.tensor_tensor(rest[:, c % 2, :], rot[:, c % 2, :], part(c, 0),
                                  ALU.subtract).then_inc(rest1, 1)

            dve.wait_ge(rope_in, 16)
            for c in range(8):
                r, w = divmod(c, 2)
                cols = slice((r % 2) * HALF, (r % 2 + 1) * HALF)
                dve.wait_ge(projected, c + 1)
                for m in range(2):
                    dve.tensor_tensor(prod[:, c % 2, m, :], round_bank(r, 2 * w + m), rope_sb[:, m, cols],
                                      ALU.mult).then_inc(products, 1)
                dve.wait_ge(products, 2 * c + 2)
                if c >= 2 and c % 2 == 0:
                    dve.wait_ge(part_again, c - 1)
                dve.tensor_tensor(rot[:, c % 2, :], prod[:, c % 2, 0, :], prod[:, c % 2, 1, :],
                                  ALU.add).then_inc(rotated, 1)
                if c >= 1:
                    leave(c - 1)
            leave(7)

            def maximum(i, u):
                t, heads = UNITS[u]
                wait(dve, a_filled, i * NUNITS + u + 1, alone=True)
                for j in heads:
                    at, w = unit_place(u, j)
                    col = j * 4 + t % 4
                    last = dve.tensor_tensor_reduce(masked_scores[:, u % 2, at:at + w],
                                                    psA[:, (u % 2) * SEQ + at:(u % 2) * SEQ + at + w],
                                                    cmask[:, SEQ - w:SEQ], 1.0, LOWEST, ALU.add, ALU.max,
                                                    mx[:, t // 4, col:col + 1])
                last.then_inc(a_drained, 1)

            def turn_shifts(i, hf):
                wait(dve, shift_split, 2 * i + hf + 1)
                wait(dve, shift_in[hf], i * (16 * SHIFT_DMAS))
                dve.transpose(shiftsT[:, hf, :], shifts[:, hf, :]).then_inc(shift_turned[hf], 1)

            def body(i, more):
                if not more:
                    turn_shifts(i, 1)
                    return
                for u in range(NUNITS):
                    if u == 1:
                        turn_shifts(i, 1)
                    if u == HALF_UNITS + 2:
                        turn_shifts(i + 1, 0)
                    maximum(i + 1, u)

            dve.wait_ge(cmask_ready, 2)
            for u in range(NUNITS):
                if u == HALF_UNITS + 2:
                    turn_shifts(0, 0)
                maximum(0, u)
            body(0, True)
            with dve.Fori(1, QUADS - 1) as i:
                body(i, True)
            body(QUADS - 1, False)

            dve.wait_ge(xb_ready, 1)

            def normalise_heads(g):
                dve.wait_ge(o_turned, g + 1)
                both = psA[:, 0:SEQ] if g < GROUPS - 1 else psB[:, 0:SEQ]
                heads = both.rearrange("p (h c) -> p h c", c=32)
                if g >= 2:
                    dve.wait_ge(on_turned, g - 1)
                dve.reciprocal(rden[:, g % 2, :], heads[:, :, DH]).then_inc(recip_ready, 1)
                dve.wait_ge(recip_ready, g + 1)
                dve.tensor_tensor(on[:, g % 2, :].rearrange("p (h d) -> p h d", d=DH), heads[:, :, 0:DH],
                                  rden[:, g % 2, :].unsqueeze(2).to_broadcast([P, 2 * HEADS, DH]),
                                  ALU.mult).then_inc(on_ready, 1)

            def result(g):
                dve.wait_ge(y_filled, g + 1)
                dve.tensor_tensor(y_sb[:, 2 * g:2 * g + 2, :].rearrange("p t d -> p (t d)"),
                                  result_bank(g, 3)[:, 0:2 * P],
                                  x_sb[:, 2 * g:2 * g + 2, :].rearrange("p t d -> p (t d)"),
                                  ALU.add).then_inc(y_ready, 1)

            for g in range(GROUPS - 2):
                normalise_heads(g)
                result(g)
            normalise_heads(GROUPS - 2)
            normalise_heads(GROUPS - 1)
            result(GROUPS - 2)
            result(GROUPS - 1)

        @block.tensor
        def _(pe):
            pe.wait_ge(ident_ready, 2)

            def turn_rows(g):
                for t in range(4 * g, 4 * g + 4):
                    pe.wait_ge(xn_ready, t + 1)
                    mm = pe.transpose(bank_a(g)[:, (t % 4) * P:(t % 4 + 1) * P], xn[:, t, :], ident[:, :])
                mm.then_inc(xn_turned, 1)

            def project_round(r):
                pe.wait_ge(xnT_ready, 4 if r else 1)
                if r >= 2:
                    pe.wait_ge(products, 8 * (r - 1) - 4)
                for w in range(4):
                    mm = pe.matmul(round_bank(r, w), w_sb[:, w, :], xnT[:, r * HALF:(r + 1) * HALF],
                                   start=True, stop=True)
                    if w % 2:
                        mm.then_inc(projected, 1)

            turn_rows(0)
            pe.wait_ge(wq_scaled, 1)
            project_round(0)
            for g in range(1, 4):
                turn_rows(g)
            for r in range(1, 4):
                project_round(r)
            pe.wait_ge(products, 12)
            for t in range(TILES):
                mm = pe.matmul(round_bank(4, t // 4)[:, (t % 4) * P:(t % 4 + 1) * P], xnT[:, t * P:(t + 1) * P],
                               w_sb[:, 4, :], start=True, stop=True)
                if t % 4 == 3:
                    mm.then_inc(v_projected, 1)

            def stack(tensor, i, j, start, size):
                half, at = divmod(start, HALF)
                return tensor[:, bass.ds(i % SLOTS, 1), half, j, at:at + size].rearrange("p o t -> p (o t)")

            def scores(i, u):
                t, heads = UNITS[u]
                if u in (0, HALF_UNITS):
                    wait(pe, stack_in[u // HALF_UNITS], (i + 1) * (16 * STACK_DMAS))
                wait(pe, a_drained, i * NUNITS + u - 1)
                for j in heads:
                    at, w = unit_place(u, j)
                    for k in range(0, w, HALF):
                        mm = pe.matmul(psA[:, (u % 2) * SEQ + at + k:(u % 2) * SEQ + at + min(k + HALF, w)],
                                       stack(qs, i, j, t * P, P), stack(ks, i, j, k, min(HALF, w - k)),
                                       start=True, stop=True)
                mm.then_inc(a_filled, 1)

            def shifted(i, s, k):
                kind, hf, kb = STEPS[s]
                n = BANK_END[s] - BANKS[s] + k
                out_bank = bank_b(n % B_RING)
                wait(pe, exp_done, i * NBANKS + n - B_RING + 1)
                if k == 0 and s == FIRST[hf]:
                    wait(pe, shift_in[hf], (i + 1) * (16 * SHIFT_DMAS))
                if kind in (FULL, D0):
                    pieces = [(0, k, kb, 0)]
                elif kind == D1:
                    pieces = [(0, k, 4 * hf + 1, P), (3 * P, k, 4 * hf + 3, 3 * P)]
                else:
                    pieces = [(0, 2 * k, 4 * hf + 2, 2 * P), (2 * P, 2 * k + 1, 4 * hf + 2, 2 * P)]
                for col, j, b, q0 in pieces:
                    size = HALF - q0
                    mm = pe.matmul(out_bank[:, col:col + size], stack(ks, i, j, b * P, P),
                                   stack(qs, i, j, hf * HALF + q0, size), start=True, stop=True)
                mm.then_inc(b_filled, 1)

            def values(i, s):
                kind, hf, kb = STEPS[s]
                if kind == FULL:
                    wait(pe, exp_done, i * NBANKS + BANK_END[s])
                else:
                    wait(pe, masked, i * NMASKS + MASK_END[s])
                if s == FIRST[hf]:
                    wait(pe, ot_saved, 2 * i + hf)
                if s == 0 or s == 7:
                    wait(pe, va_ready, 2 * i + (s == 7) + 1)
                if kind in (FULL, D0):
                    pieces = [(kb, 0, HALF, 0)]
                elif kind == D1:
                    pieces = [(4 * hf + 1, P, HALF, 0), (4 * hf + 3, 3 * P, HALF, 3 * P)]
                else:
                    pieces = [(4 * hf + 2, 2 * P, 256, 0)]
                for b, q0, pitch, at in pieces:
                    for j in range(QUAD):
                        src = ring[:, s % P_RING, j * pitch + at:j * pitch + at + HALF - q0]
                        mm = pe.matmul(psV[32 * j:32 * j + 32, q0:HALF], va[:, b, j, :], src,
                                       start=(s == FIRST[hf]), stop=(s == LAST[hf]))
                mm.then_inc(pv_done, 1)

            after = units_after()

            def body(i, first, more, then=None):
                u = 0
                for s in range(NSTEPS):
                    for k in range(BANKS[s]):
                        n = BANK_END[s] - BANKS[s] + k
                        shifted(i, s, k)
                        if k == 1:
                            if s >= LAG:
                                values(i, s - LAG)
                            elif not first:
                                values(i - 1, NSTEPS + s - LAG)
                        if more:
                            for _ in range(after[n]):
                                scores(i + 1, u)
                                u += 1
                        if then:
                            then(n)

            pe.wait_ge(products, 16)
            for u in range(NUNITS):
                scores(0, u)
            pe.wait_ge(v_ready, 4)
            body(0, True, True)
            with pe.Fori(1, QUADS - 1) as i:
                body(i, False, True)

            def turn(g):
                pe.wait_ge(ot_saved, QUADS if g < 4 else 2 * QUADS - 1 if g < 6 else 2 * QUADS)
                if g == 0:
                    pe.wait_ge(a_drained, QUADS * NUNITS)
                elif g < GROUPS - 1:
                    pe.wait_ge(on_ready, g)
                b, q = divmod(2 * g, TPB)
                for m in range(2):
                    for k in range(4):
                        mm = pe.transpose(result_bank(g, m)[:, k * P:(k + 1) * P],
                                          ot[:, 4 * b + k, (q + m) * P:(q + m + 1) * P], ident[:, :])
                mm.then_inc(o_turned, 1)

            def turn_back(g):
                pe.wait_ge(on_ready, g + 1)
                if 0 < g < GROUPS - 1:
                    pe.wait_ge(onT_ready, g)
                for m in range(2):
                    mm = pe.transpose(result_bank(g, 2)[:, m * P:(m + 1) * P], on[:, g % 2, m * P:(m + 1) * P],
                                      ident[:, :])
                mm.then_inc(on_turned, 1)

            def project(g):
                pe.wait_ge(onT_ready, g + 1)
                if 0 < g < GROUPS - 1:
                    pe.wait_ge(y_ready, g)
                for m in range(2):
                    t, dst = 2 * g + m, result_bank(g, 3)[:, m * P:(m + 1) * P]
                    pe.matmul(dst, xnT[:, t * P:(t + 1) * P], w_sb[:, 6, :], start=True, stop=False)
                    mm = pe.matmul(dst, onT[:, g % 2, m * P:(m + 1) * P], w_sb[:, 5, :], start=False, stop=True)
                mm.then_inc(y_filled, 1)

            def early(n):
                if n - PROJECT in EARLY:
                    project(EARLY[n - PROJECT])
                if n - TURN_BACK in EARLY:
                    turn_back(EARLY[n - TURN_BACK])
                if n in EARLY:
                    turn(EARLY[n])

            pe.wait_ge(cb_scaled, 4)
            body(QUADS - 1, False, False, then=early)
            for s in range(NSTEPS - LAG, NSTEPS):
                values(QUADS - 1, s)
            turn(GROUPS - 2)
            turn(GROUPS - 1)
            turn_back(GROUPS - 2)
            turn_back(GROUPS - 1)
            project(GROUPS - 2)
            project(GROUPS - 1)


def rope_tables():
    powers = np.arange(0, DH, 2, dtype=np.float32) / np.float32(DH)
    freqs = (np.float32(1.0) / np.power(np.float32(10000.0), powers)).astype(np.float32)
    angles = np.outer(np.arange(SEQ, dtype=np.float32), freqs).astype(np.float32)
    cos, sin = np.cos(angles), np.sin(angles)
    table = np.empty((P, 2, SEQ), np.float32)
    for ch in range(P):
        f = (ch % DH) // 2
        table[ch, 0] = cos[:, f]
        table[ch, 1] = sin[:, f] if ch % 2 else -sin[:, f]
    return table


def kernel(L0_attn_x, L0_attn_wq, L0_attn_wk, L0_attn_wv, L0_attn_wo, L0_ffn_CB, L0_ffn_SCB, L0_ffn_bias):
    import concourse.bacc as bacc
    from concourse.bass_utils import run_bass_kernel_spmd

    swap = np.arange(P) ^ 1
    wq, wk = np.asarray(L0_attn_wq), np.asarray(L0_attn_wk)
    weights = np.stack([wq.T, wq[swap].T, wk.T, wk[swap].T, np.asarray(L0_attn_wv).T,
                        np.asarray(L0_attn_wo).T, np.asarray(L0_ffn_CB).T], axis=1)
    arrays = {
        "x": np.ascontiguousarray(L0_attn_x).reshape(BATCH * SEQ, DM),
        "weights": np.ascontiguousarray(weights),
        "rope": rope_tables(),
        "scb": np.ascontiguousarray(L0_ffn_SCB),
        "bias": np.ascontiguousarray(L0_ffn_bias),
    }
    nc = bacc.Bacc("TRN2", target_bir_lowering=False, num_devices=1)
    args = [nc.dram_tensor(n, a.shape, mybir.dt.from_np(a.dtype), kind="ExternalInput").ap() for n, a in arrays.items()]
    y = nc.dram_tensor("y", (BATCH * SEQ, DM), F32, kind="ExternalOutput").ap()
    attention_ffn_kernel(nc, *args, y)
    r = run_bass_kernel_spmd(nc, [arrays], core_ids=[0])
    return r.results[0]["y"].reshape(BATCH, SEQ, DM)
```

```python
from contextlib import ExitStack

import numpy as np
import concourse.bass as bass
from concourse import mybir

P = 128
BATCH, SEQ, DM = 2, 1024, 128
HEADS, DH = 16, 8
TILES = BATCH * SEQ // P
TPB = SEQ // P
HALF = 512
QUAD = 4
QUADS = BATCH * HEADS // QUAD
SLOTS = 3
PARTS = 3
GROUP = PARTS * DH
STACK = PARTS * GROUP
SHIFT = STACK
NSHIFT = 2
SCALE = float(1.0 / np.sqrt(np.float32(DH)))
EPS = 1e-5
LOWEST = -3.0e38
TWO_ONES = float(np.frombuffer(np.array([0x3F803F80], np.uint32).tobytes(), np.float32)[0])

F32 = mybir.dt.float32
BF16 = mybir.dt.bfloat16
ALU = mybir.AluOpType
ACT = mybir.ActivationFunctionType

FULL, D0, D1, D2 = range(4)
STEPS = [(D0, 0, 0), (D1, 0, None), (D2, 0, None)]
STEPS += [(FULL, 1, kb) for kb in range(4)]
STEPS += [(D0, 1, 4), (D1, 1, None), (D2, 1, None)]
NSTEPS = len(STEPS)
BANKS = [2 if kind == D2 else 4 for kind, _, _ in STEPS]
BANK_END = [sum(BANKS[:s + 1]) for s in range(NSTEPS)]
NBANKS = sum(BANKS)
MASKS = [{FULL: 0, D0: 1, D1: 2, D2: 1}[kind] for kind, _, _ in STEPS]
MASK_END = [sum(MASKS[:s + 1]) for s in range(NSTEPS)]
NMASKS = sum(MASKS)
LAST = {0: 2, 1: 9}
FIRST = {0: 0, 1: 3}
LAG = 2
B_RING = 3
P_RING = 5
UNITS = []
for t in range(TPB):
    together = {0: 4, 1: 4, 2: 2, 3: 2}.get(t, 1)
    UNITS += [(t, range(j, j + together)) for j in range(0, QUAD, together)]
NUNITS = len(UNITS)
HALF_UNITS = sum(t < TPB // 2 for t, _ in UNITS)


UNIT_BANK = [1, 2, 4, 6, 7, 9, 10, 12, 14, 15, 15, 19, 20, 21, 23, 24, 25, 26, 27, 30, 32, 34]
VALUE_BANK = [9, 14, 17, 20, 23, 25, 31, 35, 39, 42]
LAST_VALUE_BANK = [9, 12, 14, 17, 20, 24, 28, 33, 37, 39]


def unit_place(u, j):
    t, heads = UNITS[u]
    w = (t + 1) * P
    pitch = HALF if len(heads) == 2 else 256 if t == 1 else w
    return (j - heads[0]) * pitch, w


GROUPS = TILES // 2
EARLY = {1: 0, 6: 1, 12: 2, 18: 3, 24: 4, 29: 5}
TURN_BACK, PROJECT = 4, 6


TASKS = [("late", 4), ("late", 5), ("v", 0), ("v", 1), ("late", 6), ("late", 7), ("ffn", 0), ("ffn", 1)]
FIRST_TASKS = 3
TASK_AFTER = {1: (3, 0), 2: (3, 1), 5: (4, 0), 6: (4, 1), 7: (5, 0), 8: (5, 1), 11: (6, 0), 12: (6, 1), 13: (7, 0), 14: (7, 1)}
LATE = 4


def attention_ffn_kernel(nc, x, weights, rope, scb, bias, out):
    ctx = ExitStack()
    with ctx:
        def sb(name, shape, dt):
            return ctx.enter_context(nc.sbuf_tensor(name, shape, dt))

        def sem(name):
            return ctx.enter_context(nc.semaphore(name))

        x_sb = sb("x_sb", [P, TILES, DM], F32)
        xn = sb("xn", [P, TILES, DM], F32)
        xnT = sb("xnT", [P, TILES * P], F32)
        w_sb = sb("w_sb", [P, 7, DM], F32)
        rope_sb = sb("rope_sb", [P, 2, SEQ], F32)
        scb_sb = sb("scb_sb", [P, DM], F32)
        bias_sb = sb("bias_sb", [P, DM], F32)
        stats = sb("stats", [P, TILES, 6], F32)
        mv = sb("mv", [P, TILES, 2], F32)
        var_eps = sb("var_eps", [P, TILES], F32)
        exponent = sb("exponent", [P, TILES], F32)
        rstd = sb("rstd", [P, TILES], F32)
        ident = sb("ident", [P, P], F32)
        cmask = sb("cmask", [P, SEQ], F32)
        prod = sb("prod", [P, 2, 2, HALF], F32)
        rot = sb("rot", [P, 2, HALF], F32)
        rest = sb("rest", [P, 2, HALF], F32)
        v_all = sb("v_all", [P, TILES, DM], F32)
        va = sb("va", [P, TPB, QUAD, 32], F32)
        qs = sb("qs", [P, SLOTS, 2, QUAD, HALF], BF16)
        ks = sb("ks", [P, SLOTS, 2, QUAD, HALF], BF16)
        ring = sb("ring", [P, P_RING, QUAD * HALF], F32)
        mx = sb("mx", [P, 2, 16], F32)
        mrest = sb("mrest", [P, 2, 16], F32)
        shifts = sb("shifts", [P, 2, 32], BF16)
        shiftsT = sb("shiftsT", [P, 2, 32], BF16)
        ot = sb("ot", [P, QUADS, SEQ], F32)
        rden = sb("rden", [P, 2, 2 * HEADS], F32)
        on = sb("on", [P, 2, 2 * DM], F32)
        onT = sb("onT", [P, 2, 2 * DM], F32)
        parts = ot[:, QUADS // 2:, :].rearrange("p a b -> p (a b)").bitcast(BF16)\
            .rearrange("p (r n t) -> p r n t", r=2, t=HALF)

        def part(c, n):
            return parts[:, (c // 2) % 2, PARTS * (c % 2) + n, :]

        masked_scores = prod[:, :, :, :].rearrange("p u m q -> p u (m q)")
        y_sb = xn

        psA = ctx.enter_context(nc.psum_tensor("psA", [P, 4 * HALF], F32))
        psB = ctx.enter_context(nc.psum_tensor("psB", [P, B_RING * HALF], F32))
        psV = ctx.enter_context(nc.psum_tensor("psV", [P, HALF], F32))

        scratch = (nc.dram_tensor("q_scratch", [HEADS, PARTS + 2, DH, BATCH * SEQ], BF16),
                   nc.dram_tensor("k_scratch", [HEADS, PARTS, DH, BATCH * SEQ], BF16))

        def bank_a(n):
            return psA[:, n * HALF:(n + 1) * HALF]

        def bank_b(n):
            return psB[:, n * HALF:(n + 1) * HALF]

        def round_bank(r, w):
            if r % 2:
                return bank_a(w)
            return bank_b(w) if w < 3 else psV[:, :]

        def task_bank(n, m):
            return round_bank(0, 2 * (n % 2) + m)

        def turn_bank(g):
            return bank_a(g) if g < 2 else task_bank(1, g - 2)

        def raw(c, m):
            at = 8 * (c % 2) + 4 * m
            return xn[:, at:at + 4, :].rearrange("p t d -> p (t d)")

        ffn_sb = ot[:, 2:4, :]

        def result_bank(g, n):
            if g < GROUPS - 2:
                return bank_a(n)
            late = g - (GROUPS - 2)
            return bank_a(2 * late + n) if n < 2 else round_bank(0, 2 * late + n - 2)

        x_in = [sem(f"x_in{g}") for g in range(4)]
        w_in = sem("w_in")
        rope_in = sem("rope_in")
        vec_in = sem("vec_in")
        ident_ready = sem("ident_ready")
        cmask_ready = sem("cmask_ready")
        pads_ready = sem("pads_ready")
        wq_scaled = sem("wq_scaled")
        cb_scaled = sem("cb_scaled")
        ln_step = sem("ln_step")
        rstd_step = sem("rstd_step")
        rstd_ready = sem("rstd_ready")
        xn_ready = sem("xn_ready")
        xn_turned = sem("xn_turned")
        xnT_ready = sem("xnT_ready")
        projected = sem("projected")
        products = sem("products")
        rotated = sem("rotated")
        part1 = sem("part1")
        rest1 = sem("rest1")
        part2 = sem("part2")
        part3 = sem("part3")
        scratch_out = [sem(f"scratch_out{r}") for r in range(4)]
        pads0_ready = sem("pads0_ready")
        task_filled = sem("task_filled")
        task_saved = sem("task_saved")
        late_step = sem("late_step")
        late_rotated = sem("late_rotated")
        late_rest = sem("late_rest")
        xb_ready = sem("xb_ready")
        stack_in = [sem(f"stack_in{h}") for h in range(2)]
        a_filled = sem("a_filled")
        a_drained = sem("a_drained")
        split_step = sem("split_step")
        shift_split = sem("shift_split")
        shift_turned = [sem(f"shift_turned{h}") for h in range(2)]
        shift_in = [sem(f"shift_in{h}") for h in range(2)]
        b_filled = sem("b_filled")
        exp_done = sem("exp_done")
        masked = sem("masked")
        va_ready = sem("va_ready")
        pv_done = sem("pv_done")
        ot_saved = sem("ot_saved")
        o_turned = sem("o_turned")
        recip_ready = sem("recip_ready")
        on_ready = sem("on_ready")
        on_turned = sem("on_turned")
        onT_ready = sem("onT_ready")
        y_filled = sem("y_filled")
        y_ready = sem("y_ready")
        y_out = sem("y_out")
        passed = sem("passed")

        def wait(eng, semaphore, value, alone=False):
            if isinstance(value, int) and value <= 0:
                return
            eng.wait_ge(semaphore, value)
            if alone and not isinstance(value, int):
                eng.sem_inc(passed, 1)

        def stacks_loaded(n):
            return 16 * 2 * PARTS * n if isinstance(n, int) and n < SLOTS else 16 * (2 * PARTS * n + n - SLOTS)

        SHIFT_DMAS = 4
        ROUND_DMAS = 2 * PARTS + 2

        block = ctx.enter_context(nc.Block())

        @block.sync
        def _(sp):
            xv = x.rearrange("(t p) d -> p t d", p=P)
            for g in range(4):
                sp.dma_start(x_sb[:, 4 * g:4 * g + 4, :], xv[:, 4 * g:4 * g + 4, :]).then_inc(x_in[g], 16)

            def store_part(c, n):
                tok = c // 2 * HALF
                sp.wait_ge((part1, part2, part3)[n], c + 1)
                for m in (n, PARTS + n) if c % 2 == 0 and n < 2 else (n,):
                    sp.dma_start(scratch[c % 2][:, m, :, tok:tok + HALF], part(c, n)).then_inc(scratch_out[c // 2], 16)

            def store_parts(r, done=()):
                for n in range(PARTS):
                    for c in (2 * r, 2 * r + 1):
                        if (c, n) not in done:
                            store_part(c, n)

            def load_stack(i, hf):
                slot, heads, tok = i % SLOTS, (i % 4) * QUAD, (i // 4) * SEQ + hf * HALF
                for g in range(PARTS):
                    for source, first, stack in ((scratch[0], g, qs), (scratch[1], 0, ks)):
                        sp.dma_start(stack[g * GROUP:(g + 1) * GROUP, bass.ds(slot, 1), hf, :, :].rearrange("r o h t -> r (o h) t"),
                                     source[bass.ds(heads, QUAD), first:first + PARTS, :, bass.ds(tok, HALF)]
                                     .rearrange("h p d t -> (p d) h t")).then_inc(stack_in[hf], 16)
                if isinstance(i, int) and i < SLOTS:
                    return
                sp.dma_start(qs[SHIFT:SHIFT + NSHIFT, bass.ds(slot, 1), hf, :, :].rearrange("r o h t -> r (o h) t"),
                             qs[SHIFT + NSHIFT:SHIFT + 2 * NSHIFT, bass.ds(slot, 1), hf, :, :].rearrange("r o h t -> r (o h) t"))\
                    .then_inc(stack_in[hf], 16)

            def store_shifts(i, hf):
                slot = i % SLOTS
                wait(sp, shift_turned[hf], i + 1, alone=True)
                for blk in range(4):
                    dst = qs[SHIFT:SHIFT + NSHIFT, bass.ds(slot, 1), hf, :, :]
                    dst = dst.rearrange("r o h (t k q) -> r o (h t) k q", k=4, q=32)[:, :, :, blk, :]
                    sp.dma_start(dst, shiftsT[32 * blk:32 * blk + 32, hf, :]).then_inc(shift_in[hf], 16)

            store_parts(0)
            store_part(2, 0)
            sp.wait_ge(pads0_ready, 2)
            sp.wait_ge(scratch_out[0], 16 * ROUND_DMAS)
            load_stack(0, 0)
            store_parts(1, done=[(2, 0)])
            sp.wait_ge(scratch_out[1], 16 * ROUND_DMAS)
            load_stack(0, 1)
            sp.wait_ge(pads_ready, 2)
            for hf in range(2):
                sp.wait_ge(stack_in[hf], stacks_loaded(1))
                load_stack(1, hf)
            store_shifts(0, 0)
            store_parts(2)

            def body(i):
                store_shifts(i, 1)
                if isinstance(i, int):
                    sp.wait_ge(pads_ready, 4)
                for hf in range(2):
                    wait(sp, stack_in[hf], stacks_loaded(i + 2), alone=True)
                wait(sp, b_filled, i * NBANKS, alone=True)
                for hf in range(2):
                    load_stack(i + 2, hf)
                store_shifts(i + 1, 0)

            body(0)
            store_parts(3)
            for r in range(2, 4):
                sp.wait_ge(scratch_out[r], 16 * ROUND_DMAS)
            with sp.Fori(1, QUADS - 2) as i:
                body(i)
            store_shifts(6, 1)
            store_shifts(7, 0)
            store_shifts(7, 1)
            ov = out.rearrange("(t p) d -> p t d", p=P)
            for g in range(GROUPS):
                sp.wait_ge(y_ready, g + 1)
                sp.dma_start(ov[:, 2 * g:2 * g + 2, :], y_sb[:, 2 * g:2 * g + 2, :]).then_inc(y_out, 16)
            sp.wait_ge(y_out, 16 * GROUPS)

        @block.gpsimd
        def _(pool):
            pool.memset(ident[:, :], 0.0).then_inc(ident_ready, 1)
            pool.wait_ge(ident_ready, 1)
            pool.affine_select(out=ident[:, :], in_=ident[:, :], compare_op=ALU.not_equal, fill=1.0, base=0,
                               pattern=[[-1, P]], channel_multiplier=1).then_inc(ident_ready, 1)
            pool.memset(exponent[:, :], -0.5).then_inc(rstd_step, 1)

            def pads(stack, slot, value, ready):
                pool.memset(stack[:, slot, :, :, :].rearrange("p a h t -> p (a h t)").bitcast(F32), value)\
                    .then_inc(ready, 1)

            pads(qs, 0, 0.0, pads0_ready)
            pads(qs, 1, 0.0, pads_ready)
            for g in range(4):
                bt = slice(4 * g, 4 * g + 4)
                pool.wait_ge(ln_step, 2 * g + 2)
                pool.tensor_scalar(var_eps[:, bt], mv[:, bt, 1], EPS, None, ALU.add).then_inc(rstd_step, 1)
                pool.wait_ge(rstd_step, g + 2)
                pool.tensor_tensor(rstd[:, bt], var_eps[:, bt], exponent[:, bt], ALU.pow).then_inc(rstd_ready, 1)
            pads(ks, 1, TWO_ONES, pads_ready)

            def third_part(c):
                pool.wait_ge(part2, c + 1)
                if c >= LATE:
                    pool.wait_ge(scratch_out[c // 2 - 2], 16 * ROUND_DMAS)
                left = rest[:, c % 2, :] if c < LATE else raw(c, 1)
                pool.tensor_tensor(part(c, 2), left, part(c, 1), ALU.subtract).then_inc(part3, 1)

            def rotate(c):
                n, cols = c - LATE, slice((c // 2 % 2) * HALF, (c // 2 % 2 + 1) * HALF)
                pool.wait_ge(task_saved, TASKS.index(("late", c)) + 1)
                for m in range(2):
                    pool.tensor_tensor(raw(c, m), raw(c, m), rope_sb[:, m, cols], ALU.mult).then_inc(late_step, 1)
                pool.wait_ge(late_step, 2 * n + 2)
                pool.tensor_tensor(raw(c, 0), raw(c, 0), raw(c, 1), ALU.add).then_inc(late_rotated, 1)

            def leave(c):
                pool.wait_ge(part1, c + 1)
                pool.tensor_tensor(raw(c, 1), raw(c, 0), part(c, 0), ALU.subtract).then_inc(late_rest, 1)

            for c in range(LATE):
                third_part(c)
                if c == 1:
                    pool.memset(cmask[:, :], 0.0).then_inc(cmask_ready, 1)
                    pool.wait_ge(cmask_ready, 1)
                    pool.affine_select(out=cmask[:, SEQ - P:SEQ], in_=cmask[:, SEQ - P:SEQ],
                                       compare_op=ALU.is_ge, fill=LOWEST, base=0, pattern=[[-1, P]],
                                       channel_multiplier=1).then_inc(cmask_ready, 1)
            pool.wait_ge(rope_in, 16)

            def split_maxima(i, hf):
                n = 2 * i + hf
                wait(pool, a_drained, i * NUNITS + (NUNITS if hf else HALF_UNITS))
                if hf == 0:
                    wait(pool, shift_turned[0], i, alone=True)
                else:
                    wait(pool, shift_turned[1], i, alone=True)
                pool.tensor_scalar(shifts[:, hf, 0:16], mx[:, hf, :], -1.0, None, ALU.mult).then_inc(split_step, 1)
                pool.wait_ge(split_step, 2 * n + 1)
                pool.tensor_tensor(mrest[:, hf, :], mx[:, hf, :], shifts[:, hf, 0:16], ALU.add).then_inc(split_step, 1)
                wait(pool, split_step, 2 * n + 2, alone=True)
                pool.tensor_scalar(shifts[:, hf, 16:32], mrest[:, hf, :], -1.0, None, ALU.mult).then_inc(shift_split, 1)

            def copy_v(i, hf):
                tiles, ch = (i // 4) * TPB + hf * 4, (i % 4) * (QUAD * DH)
                src = v_all[:, bass.ds(tiles, 4), bass.ds(ch, QUAD * DH)].rearrange("p t (h d) -> p t h d", d=DH)
                pool.tensor_copy(va[:, hf * 4:hf * 4 + 4, :, 0:DH], src).then_inc(va_ready, 1)

            def mask(i, s):
                kind = STEPS[s][0]
                buf = ring[:, s % P_RING, :]
                wait(pool, exp_done, i * NBANKS + BANK_END[s], alone=True)
                if kind == D2:
                    views = [buf[:, 0:QUAD * 256].rearrange("p (h q) -> p h q", h=QUAD)[:, :, 0:P]]
                else:
                    blocks = buf.rearrange("p (h k q) -> p h k q", h=QUAD, k=4)
                    views = [blocks[:, :, k, :] for k in ((0,) if kind == D0 else (0, 3))]
                for view in views:
                    pool.affine_select(out=view, in_=view, compare_op=ALU.is_ge, fill=0.0, base=0,
                                       pattern=[[0, QUAD], [1, P]], channel_multiplier=-1).then_inc(masked, 1)

            def body(i, more):
                wait(pool, pv_done, i * NSTEPS - 3)
                copy_v(i, 0)
                mask(i, 0)
                mask(i, 1)
                wait(pool, pv_done, i * NSTEPS)
                copy_v(i, 1)
                mask(i, 2)
                if more:
                    split_maxima(i + 1, 0)
                if isinstance(i, int) and i == 0:
                    pads(qs, 2, 0.0, pads_ready)
                    pads(ks, 2, TWO_ONES, pads_ready)
                    add_ffn()
                mask(i, 7)
                mask(i, 8)
                if more:
                    split_maxima(i + 1, 1)
                mask(i, 9)

            def add_ffn():
                pool.wait_ge(xn_ready, TILES)
                pool.wait_ge(task_saved, TASKS.index(("ffn", 1)) + 1)
                pool.tensor_tensor(x_sb[:, :, :].rearrange("p t d -> p (t d)"),
                                   x_sb[:, :, :].rearrange("p t d -> p (t d)"),
                                   ffn_sb.rearrange("p a b -> p (a b)"), ALU.add).then_inc(xb_ready, 1)

            rotate(4)
            rotate(5)
            leave(4)
            leave(5)
            third_part(4)
            third_part(5)
            split_maxima(0, 0)
            pool.wait_ge(vec_in, 32)
            pool.wait_ge(w_in, 16)
            pool.tensor_scalar(scb_sb[:, :], scb_sb[:, :], 1.0 / 127.0, None, ALU.mult).then_inc(cb_scaled, 1)
            pool.memset(va[:, :, :, :], 0.0).then_inc(cb_scaled, 1)
            pool.wait_ge(cb_scaled, 2)
            pool.tensor_tensor(w_sb[:, 6, :], w_sb[:, 6, :], scb_sb[:, :], ALU.mult).then_inc(cb_scaled, 1)
            pool.memset(va[:, :, :, DH:DH + 1], 1.0).then_inc(cb_scaled, 1)
            rotate(6)
            rotate(7)
            leave(6)
            leave(7)
            third_part(6)
            third_part(7)
            split_maxima(0, 1)
            body(0, True)
            with pool.Fori(1, QUADS - 1) as i:
                body(i, True)
            body(QUADS - 1, False)

        @block.scalar
        def _(act):
            act.dma_start(w_sb[:, :, :], weights).then_inc(w_in, 16)
            act.dma_start(rope_sb[:, :, :], rope).then_inc(rope_in, 16)
            act.dma_start(scb_sb[:, :], scb.partition_broadcast(P)).then_inc(vec_in, 16)
            act.dma_start(bias_sb[:, :], bias.partition_broadcast(P)).then_inc(vec_in, 16)
            act.wait_ge(w_in, 16)
            act.activation(w_sb[:, 0:2, :], w_sb[:, 0:2, :], ACT.Copy, scale=SCALE).then_inc(wq_scaled, 1)

            def turned_rows(g):
                act.wait_ge(xn_turned, g + 1)
                act.activation(xnT[:, g * HALF:(g + 1) * HALF], turn_bank(g), ACT.Copy).then_inc(xnT_ready, 1)

            def parts_of(c, n):
                if c < LATE:
                    act.wait_ge((rotated, rest1)[n], c + 1)
                    source = (rot, rest)[n][:, c % 2, :]
                else:
                    act.wait_ge((late_rotated, late_rest)[n], c - LATE + 1)
                    act.wait_ge(scratch_out[c // 2 - 2], 16 * ROUND_DMAS)
                    source = raw(c, n)
                act.activation(part(c, n), source, ACT.Copy).then_inc((part1, part2)[n], 1)

            def save_task(n):
                kind, c = TASKS[n]
                act.wait_ge(task_filled, n + 1)
                if kind == "late" and c >= LATE + 2:
                    act.wait_ge(part3, c - 1)
                for m in range(2):
                    if kind == "late":
                        dst = raw(c, m)
                    elif kind == "v":
                        dst = v_all[:, 8 * c + 4 * m:8 * c + 4 * m + 4, :].rearrange("p t d -> p (t d)")
                    else:
                        dst = ffn_sb[:, c, m * HALF:(m + 1) * HALF]
                    last = act.activation(dst, task_bank(n, m), ACT.Copy)
                last.then_inc(task_saved, 1)

            turned_rows(0)
            turned_rows(1)
            for r in range(LATE // 2):
                for n in range(2):
                    parts_of(2 * r, n)
                    parts_of(2 * r + 1, n)
                if r == 0:
                    turned_rows(2)
                    turned_rows(3)
            save_task(0)
            save_task(1)
            save_task(2)
            save_task(3)
            parts_of(4, 0)
            parts_of(5, 0)
            parts_of(4, 1)
            parts_of(5, 1)
            save_task(4)
            save_task(5)
            parts_of(6, 0)
            parts_of(7, 0)
            save_task(6)
            save_task(7)
            parts_of(6, 1)
            parts_of(7, 1)

            def exps(i, s, then=None):
                wait(act, pv_done, i * NSTEPS + s - P_RING + 1)
                for n in range(BANK_END[s] - BANKS[s], BANK_END[s]):
                    k = n - (BANK_END[s] - BANKS[s])
                    wait(act, b_filled, i * NBANKS + n + 1)
                    act.activation(ring[:, s % P_RING, k * HALF:(k + 1) * HALF], bank_b(n % B_RING), ACT.Exp)\
                        .then_inc(exp_done, 1)
                    if then:
                        then(n)

            def save(i, hf):
                wait(act, pv_done, i * NSTEPS + LAST[hf] + 1)
                act.activation(ot[:, bass.ds(i, 1), hf * HALF:(hf + 1) * HALF].rearrange("p o q -> p (o q)"),
                               psV[:, :], ACT.Copy).then_inc(ot_saved, 1)

            def body(i, first):
                for s in range(NSTEPS):
                    exps(i, s)
                    if s == LAG - 1 and not first:
                        save(i - 1, 1)
                    if s == LAST[0] + LAG:
                        save(i, 0)

            def copy_turned(g):
                act.wait_ge(on_turned, g + 1)
                if g >= 2:
                    act.wait_ge(y_filled, g - 1)
                act.activation(onT[:, g % 2, :], result_bank(g, 2)[:, 0:2 * P], ACT.Copy).then_inc(onT_ready, 1)

            body(0, True)
            with act.Fori(1, QUADS - 1) as i:
                body(i, False)
            last = QUADS - 1

            def beside(n):
                if n == VALUE_BANK[LAST[1]] - NBANKS + 1:
                    save(last - 1, 1)
                if n == LAST_VALUE_BANK[LAST[0]] + 1:
                    save(last, 0)
                if n - TURN_BACK in EARLY:
                    copy_turned(EARLY[n - TURN_BACK])

            for s in range(NSTEPS):
                exps(last, s, then=beside)
            save(last, 1)
            for g in range(len(EARLY), GROUPS):
                copy_turned(g)

        @block.vector
        def _(dve):
            def statistics(g):
                dve.wait_ge(x_in[g], 16)
                for t in range(4 * g, 4 * g + 4):
                    last = dve.bn_stats(stats[:, t, :], x_sb[:, t, :])
                last.then_inc(ln_step, 1)
                dve.wait_ge(ln_step, 2 * g + 1)
                for t in range(4 * g, 4 * g + 4):
                    last = dve.bn_aggr(mv[:, t, :], stats[:, t, :])
                last.then_inc(ln_step, 1)

            def normalise(g):
                dve.wait_ge(rstd_ready, g + 1)
                for t in range(4 * g, 4 * g + 4):
                    dve.tensor_scalar(xn[:, t, :], x_sb[:, t, :], mv[:, t, 0:1], rstd[:, t:t + 1],
                                      ALU.subtract, ALU.mult).then_inc(xn_ready, 1)

            dve.memset(ks[:, 0, :, :, :].rearrange("p a h t -> p (a h t)").bitcast(F32), TWO_ONES)\
                .then_inc(pads0_ready, 1)
            statistics(0)
            statistics(1)
            normalise(0)
            normalise(1)
            statistics(2)
            statistics(3)
            normalise(2)

            def leave(c):
                dve.wait_ge(part1, c + 1)
                if c >= 2:
                    dve.wait_ge(part3, c - 1)
                dve.tensor_tensor(rest[:, c % 2, :], rot[:, c % 2, :], part(c, 0),
                                  ALU.subtract).then_inc(rest1, 1)

            dve.wait_ge(rope_in, 16)
            for c in range(LATE):
                if c == 2:
                    normalise(3)
                r, w = divmod(c, 2)
                cols = slice((r % 2) * HALF, (r % 2 + 1) * HALF)
                dve.wait_ge(projected, c + 1)
                for m in range(2):
                    dve.tensor_tensor(prod[:, c % 2, m, :], round_bank(r, 2 * w + m), rope_sb[:, m, cols],
                                      ALU.mult).then_inc(products, 1)
                dve.wait_ge(products, 2 * c + 2)
                dve.tensor_tensor(rot[:, c % 2, :], prod[:, c % 2, 0, :], prod[:, c % 2, 1, :],
                                  ALU.add).then_inc(rotated, 1)
                if c % 2:
                    leave(c - 1)
                    leave(c)

            def maximum(i, u):
                t, heads = UNITS[u]
                wait(dve, a_filled, i * NUNITS + u + 1, alone=True)
                for j in heads:
                    at, w = unit_place(u, j)
                    col = j * 4 + t % 4
                    last = dve.tensor_tensor_reduce(masked_scores[:, u % 2, at:at + w],
                                                    psA[:, (u % 2) * SEQ + at:(u % 2) * SEQ + at + w],
                                                    cmask[:, SEQ - w:SEQ], 1.0, LOWEST, ALU.add, ALU.max,
                                                    mx[:, t // 4, col:col + 1])
                last.then_inc(a_drained, 1)

            def turn_shifts(i, hf):
                wait(dve, shift_split, 2 * i + hf + 1)
                wait(dve, shift_in[hf], i * (16 * SHIFT_DMAS))
                dve.transpose(shiftsT[:, hf, :], shifts[:, hf, :]).then_inc(shift_turned[hf], 1)

            def body(i, more):
                if not more:
                    turn_shifts(i, 1)
                    return
                for u in range(NUNITS):
                    if u == 1:
                        turn_shifts(i, 1)
                    if u == HALF_UNITS + 2:
                        turn_shifts(i + 1, 0)
                    maximum(i + 1, u)

            dve.wait_ge(cmask_ready, 2)
            for u in range(NUNITS):
                if u == HALF_UNITS + 2:
                    turn_shifts(0, 0)
                maximum(0, u)
            body(0, True)
            with dve.Fori(1, QUADS - 1) as i:
                body(i, True)
            body(QUADS - 1, False)

            dve.wait_ge(part3, 8)

            def normalise_heads(g):
                dve.wait_ge(o_turned, g + 1)
                both = psA[:, 0:SEQ] if g < GROUPS - 1 else psA[:, SEQ:2 * SEQ]
                heads = both.rearrange("p (h c) -> p h c", c=32)
                if g >= 2:
                    dve.wait_ge(on_turned, g - 1)
                dve.reciprocal(rden[:, g % 2, :], heads[:, :, DH]).then_inc(recip_ready, 1)
                dve.wait_ge(recip_ready, g + 1)
                dve.tensor_tensor(on[:, g % 2, :].rearrange("p (h d) -> p h d", d=DH), heads[:, :, 0:DH],
                                  rden[:, g % 2, :].unsqueeze(2).to_broadcast([P, 2 * HEADS, DH]),
                                  ALU.mult).then_inc(on_ready, 1)

            def result(g):
                dve.wait_ge(y_filled, g + 1)
                dve.tensor_tensor(y_sb[:, 2 * g:2 * g + 2, :].rearrange("p t d -> p (t d)"),
                                  result_bank(g, 3)[:, 0:2 * P],
                                  x_sb[:, 2 * g:2 * g + 2, :].rearrange("p t d -> p (t d)"),
                                  ALU.add).then_inc(y_ready, 1)

            for g in range(GROUPS - 2):
                normalise_heads(g)
                if g == 0:
                    dve.wait_ge(xb_ready, 1)
                    dve.wait_ge(vec_in, 32)
                    dve.tensor_tensor(x_sb[:, :, :], x_sb[:, :, :],
                                      bias_sb[:, :].unsqueeze(1).to_broadcast([P, TILES, DM]),
                                      ALU.add).then_inc(xb_ready, 1)
                    dve.wait_ge(xb_ready, 2)
                result(g)
            normalise_heads(GROUPS - 2)
            normalise_heads(GROUPS - 1)
            result(GROUPS - 2)
            result(GROUPS - 1)

        @block.tensor
        def _(pe):
            pe.wait_ge(ident_ready, 2)

            def turn_rows(g):
                for t in range(4 * g, 4 * g + 4):
                    pe.wait_ge(xn_ready, t + 1)
                    mm = pe.transpose(turn_bank(g)[:, (t % 4) * P:(t % 4 + 1) * P], xn[:, t, :], ident[:, :])
                mm.then_inc(xn_turned, 1)

            def project_round(r):
                pe.wait_ge(xnT_ready, r + 1)
                for w in range(4):
                    mm = pe.matmul(round_bank(r, w), w_sb[:, w, :], xnT[:, r * HALF:(r + 1) * HALF],
                                   start=True, stop=True)
                    if w % 2:
                        mm.then_inc(projected, 1)

            turn_rows(0)
            turn_rows(1)
            pe.wait_ge(wq_scaled, 1)
            project_round(0)
            project_round(1)
            pe.wait_ge(products, 4)
            turn_rows(2)
            turn_rows(3)

            def task(n, m):
                kind, c = TASKS[n]
                if m == 0:
                    pe.wait_ge(xnT_ready, 4 if n else 3)
                    if n >= 2:
                        pe.wait_ge(task_saved, n - 1)
                    if kind == "ffn":
                        pe.wait_ge(cb_scaled, 4)
                if kind == "late":
                    mm = pe.matmul(task_bank(n, m), w_sb[:, 2 * (c % 2) + m, :],
                                   xnT[:, (c // 2) * HALF:(c // 2 + 1) * HALF], start=True, stop=True)
                else:
                    for t in range(4):
                        at = (TPB * c + 4 * m + t) * P
                        mm = pe.matmul(task_bank(n, m)[:, t * P:(t + 1) * P], xnT[:, at:at + P],
                                       w_sb[:, 4 if kind == "v" else 6, :], start=True, stop=True)
                if m == 1:
                    mm.then_inc(task_filled, 1)

            def stack(tensor, i, j, start, size):
                half, at = divmod(start, HALF)
                return tensor[:, bass.ds(i % SLOTS, 1), half, j, at:at + size].rearrange("p o t -> p (o t)")

            def scores(i, u):
                t, heads = UNITS[u]
                if u in (0, HALF_UNITS):
                    wait(pe, stack_in[u // HALF_UNITS], stacks_loaded(i + 1))
                wait(pe, a_drained, i * NUNITS + u - 1)
                for j in heads:
                    at, w = unit_place(u, j)
                    for k in range(0, w, HALF):
                        mm = pe.matmul(psA[:, (u % 2) * SEQ + at + k:(u % 2) * SEQ + at + min(k + HALF, w)],
                                       stack(qs, i, j, t * P, P), stack(ks, i, j, k, min(HALF, w - k)),
                                       start=True, stop=True)
                mm.then_inc(a_filled, 1)

            def shifted(i, s, k):
                kind, hf, kb = STEPS[s]
                n = BANK_END[s] - BANKS[s] + k
                out_bank = bank_b(n % B_RING)
                wait(pe, exp_done, i * NBANKS + n - B_RING + 1)
                if k == 0 and s == FIRST[hf]:
                    wait(pe, shift_in[hf], (i + 1) * (16 * SHIFT_DMAS))
                if kind in (FULL, D0):
                    pieces = [(0, k, kb, 0)]
                elif kind == D1:
                    pieces = [(0, k, 4 * hf + 1, P), (3 * P, k, 4 * hf + 3, 3 * P)]
                else:
                    pieces = [(0, 2 * k, 4 * hf + 2, 2 * P), (2 * P, 2 * k + 1, 4 * hf + 2, 2 * P)]
                for col, j, b, q0 in pieces:
                    size = HALF - q0
                    mm = pe.matmul(out_bank[:, col:col + size], stack(ks, i, j, b * P, P),
                                   stack(qs, i, j, hf * HALF + q0, size), start=True, stop=True)
                mm.then_inc(b_filled, 1)

            def values(i, s):
                kind, hf, kb = STEPS[s]
                if kind == FULL:
                    wait(pe, exp_done, i * NBANKS + BANK_END[s])
                else:
                    wait(pe, masked, i * NMASKS + MASK_END[s])
                if s == FIRST[hf]:
                    wait(pe, ot_saved, 2 * i + hf)
                if s == 0 or s == 7:
                    wait(pe, va_ready, 2 * i + (s == 7) + 1)
                if kind in (FULL, D0):
                    pieces = [(kb, 0, HALF, 0)]
                elif kind == D1:
                    pieces = [(4 * hf + 1, P, HALF, 0), (4 * hf + 3, 3 * P, HALF, 3 * P)]
                else:
                    pieces = [(4 * hf + 2, 2 * P, 256, 0)]
                for b, q0, pitch, at in pieces:
                    for j in range(QUAD):
                        src = ring[:, s % P_RING, j * pitch + at:j * pitch + at + HALF - q0]
                        mm = pe.matmul(psV[32 * j:32 * j + 32, q0:HALF], va[:, b, j, :], src,
                                       start=(s == FIRST[hf]), stop=(s == LAST[hf]))
                mm.then_inc(pv_done, 1)

            def body(i, first, more, then=None):
                for s in range(NSTEPS):
                    for k in range(BANKS[s]):
                        n = BANK_END[s] - BANKS[s] + k
                        shifted(i, s, k)
                        if more:
                            for u in range(NUNITS):
                                if UNIT_BANK[u] == n:
                                    scores(i + 1, u)
                        for v in range(NSTEPS):
                            if (VALUE_BANK if more else LAST_VALUE_BANK)[v] == n:
                                values(i, v)
                            elif VALUE_BANK[v] == NBANKS + n and not first:
                                values(i - 1, v)
                        if then:
                            then(n)

            for n in range(FIRST_TASKS):
                for m in range(2):
                    task(n, m)
            pe.wait_ge(products, 8)
            for u in range(NUNITS):
                scores(0, u)
                if u in TASK_AFTER:
                    task(*TASK_AFTER[u])
            pe.wait_ge(task_saved, len(TASKS))
            body(0, True, True)
            with pe.Fori(1, QUADS - 1) as i:
                body(i, False, True)

            def turn(g, m, quads=range(4)):
                b, q = divmod(2 * g, TPB)
                if m == 0 and 0 in quads:
                    if g == 0:
                        pe.wait_ge(a_drained, QUADS * NUNITS)
                    elif g < GROUPS - 1:
                        pe.wait_ge(on_ready, g)
                    else:
                        pe.wait_ge(onT_ready, GROUPS - 2)
                        pe.wait_ge(y_ready, GROUPS - 2)
                if m == 0:
                    saved = 4 * b + quads[-1] + 1
                    pe.wait_ge(ot_saved, 2 * saved - (q < 4))
                for k in quads:
                    mm = pe.transpose(result_bank(g, m)[:, k * P:(k + 1) * P],
                                      ot[:, 4 * b + k, (q + m) * P:(q + m + 1) * P], ident[:, :])
                if m == 1 and 3 in quads:
                    mm.then_inc(o_turned, 1)

            def turn_back(g):
                pe.wait_ge(on_ready, g + 1)
                if 0 < g < GROUPS - 2:
                    pe.wait_ge(onT_ready, g)
                for m in range(2):
                    mm = pe.transpose(result_bank(g, 2)[:, m * P:(m + 1) * P], on[:, g % 2, m * P:(m + 1) * P],
                                      ident[:, :])
                mm.then_inc(on_turned, 1)

            def project(g):
                pe.wait_ge(onT_ready, g + 1)
                if 0 < g < GROUPS - 2:
                    pe.wait_ge(y_ready, g)
                for m in range(2):
                    mm = pe.matmul(result_bank(g, 3)[:, m * P:(m + 1) * P], onT[:, g % 2, m * P:(m + 1) * P],
                                   w_sb[:, 5, :], start=True, stop=True)
                mm.then_inc(y_filled, 1)

            def early(n):
                if n - PROJECT in EARLY:
                    project(EARLY[n - PROJECT])
                if n - TURN_BACK in EARLY:
                    turn_back(EARLY[n - TURN_BACK])
                for m in range(2):
                    if n - m in EARLY:
                        turn(EARLY[n - m], m)
                    if n == NBANKS - 2 + m:
                        turn(GROUPS - 2, m, range(3))

            pe.wait_ge(cb_scaled, 4)
            body(QUADS - 1, False, False, then=early)
            values(QUADS - 1, NSTEPS - 2)
            for m in range(2):
                turn(GROUPS - 1, m, range(3))
            values(QUADS - 1, NSTEPS - 1)
            for g in (GROUPS - 2, GROUPS - 1):
                for m in range(2):
                    turn(g, m, range(3, 4))
            turn_back(GROUPS - 2)
            turn_back(GROUPS - 1)
            project(GROUPS - 2)
            project(GROUPS - 1)


def rope_tables():
    powers = np.arange(0, DH, 2, dtype=np.float32) / np.float32(DH)
    freqs = (np.float32(1.0) / np.power(np.float32(10000.0), powers)).astype(np.float32)
    angles = np.outer(np.arange(SEQ, dtype=np.float32), freqs).astype(np.float32)
    cos, sin = np.cos(angles), np.sin(angles)
    table = np.empty((P, 2, SEQ), np.float32)
    for ch in range(P):
        f = (ch % DH) // 2
        table[ch, 0] = cos[:, f]
        table[ch, 1] = sin[:, f] if ch % 2 else -sin[:, f]
    return table


def kernel(L0_attn_x, L0_attn_wq, L0_attn_wk, L0_attn_wv, L0_attn_wo, L0_ffn_CB, L0_ffn_SCB, L0_ffn_bias):
    import concourse.bacc as bacc
    from concourse.bass_utils import run_bass_kernel_spmd

    swap = np.arange(P) ^ 1
    wq, wk = np.asarray(L0_attn_wq), np.asarray(L0_attn_wk)
    weights = np.stack([wq.T, wq[swap].T, wk.T, wk[swap].T, np.asarray(L0_attn_wv).T,
                        np.asarray(L0_attn_wo).T, np.asarray(L0_ffn_CB).T], axis=1)
    arrays = {
        "x": np.ascontiguousarray(L0_attn_x).reshape(BATCH * SEQ, DM),
        "weights": np.ascontiguousarray(weights),
        "rope": rope_tables(),
        "scb": np.ascontiguousarray(L0_ffn_SCB),
        "bias": np.ascontiguousarray(L0_ffn_bias),
    }
    nc = bacc.Bacc("TRN2", target_bir_lowering=False, num_devices=1)
    args = [nc.dram_tensor(n, a.shape, mybir.dt.from_np(a.dtype), kind="ExternalInput").ap() for n, a in arrays.items()]
    y = nc.dram_tensor("y", (BATCH * SEQ, DM), F32, kind="ExternalOutput").ap()
    attention_ffn_kernel(nc, *args, y)
    r = run_bass_kernel_spmd(nc, [arrays], core_ids=[0])
    return r.results[0]["y"].reshape(BATCH, SEQ, DM)
```
